# Optimizing a Trainium2 kernel written in Bass

```python
import numpy as np
import jax
import jax.numpy as jnp

def _softmax(x, axis=-1):
    return jax.nn.softmax(x, axis=axis)

def _gelu(x):
    return jax.nn.gelu(x, approximate=True)

def _silu(x):
    return jax.nn.silu(x)

def _sigmoid(x):
    return jax.nn.sigmoid(x)

def _layernorm(x, axis=-1, eps=1e-05):
    m = jnp.mean(x, axis=axis, keepdims=True)
    v = jnp.var(x, axis=axis, keepdims=True)
    return (x - m) / jnp.sqrt(v + eps)

def _scatter_add(tgt, idx, src, axis=0):
    return tgt.at[idx].add(src)

def _segment_sum(src, seg, n):
    return jax.ops.segment_sum(src, seg, n)
kernel_name = 'mk_gnn_resnorm_d4_gnn_r8_7e25ef'

def setup_inputs(seed: int=0):
    np.random.seed(seed)
    _w = jnp.asarray

    def _rec_inputs():
        import jax
        import jax.numpy as jnp
        _gk = jax.random.key(seed)
        x = -0.000202 + 1 * jax.random.normal(jax.random.fold_in(_gk, 1), (6250, 64), jnp.float32)
        _s = jax.random.randint(jax.random.fold_in(_gk, 2), (100000,), 0, 6250, jnp.int32)
        _d = jax.random.randint(jax.random.fold_in(_gk, 3), (100000,), 0, 6250, jnp.int32)
        _loop = jnp.arange(6250, dtype=jnp.int32)
        src = jnp.concatenate([_s, _d, _loop])
        dst = jnp.concatenate([_d, _s, _loop])
        _o = jnp.argsort(dst, stable=True)
        src = src[_o]
        dst = dst[_o]
        edge_attr_32 = -5.16925e-05 + 1.00005 * jax.random.normal(jax.random.fold_in(_gk, 13), (206250, 32), jnp.float32)
        edge_weight = 0.000452788 + 0.999756 * jax.random.normal(jax.random.fold_in(_gk, 15), (206250,), jnp.float32)
        edge_weight_n2 = 0.000452788 + 0.999756 * jax.random.normal(jax.random.fold_in(_gk, 16), (206250,), jnp.float32)
        return (x, src, dst, edge_attr_32, edge_weight, edge_weight_n2)
    x, src, dst, edge_attr_32, edge_weight, edge_weight_n2 = _rec_inputs()

    def _L0_gnn_setup():
        import jax, jax.numpy as jnp
        import numpy as np
        N = 12500
        E = 200000
        D_IN = 64
        D_OUT = 64

        def _spmm(w, src, dst, h, n):
            return jax.ops.segment_sum(w[:, None] * h[src], dst, num_segments=n)
        key = jax.random.key(seed)
        ks = jax.random.split(key, 12)
        stdv = 1.0 / np.sqrt(D_OUT)
        inp = {'x': jax.random.normal(ks[0], (N, D_IN), dtype=jnp.float32), 'w_low': jax.random.uniform(ks[1], (E,), dtype=jnp.float32), 'w_high': jax.random.normal(ks[2], (E,), dtype=jnp.float32), 'W_low': jax.random.uniform(ks[3], (D_IN, D_OUT), jnp.float32, -stdv, stdv), 'W_high': jax.random.uniform(ks[4], (D_IN, D_OUT), jnp.float32, -stdv, stdv), 'W_mlp': jax.random.uniform(ks[5], (D_IN, D_OUT), jnp.float32, -stdv, stdv), 'av_low': jax.random.normal(ks[6], (D_OUT, 1), dtype=jnp.float32), 'av_high': jax.random.normal(ks[7], (D_OUT, 1), dtype=jnp.float32), 'av_mlp': jax.random.normal(ks[8], (D_OUT, 1), dtype=jnp.float32), 'att_vec': jax.random.normal(ks[9], (3, 3), dtype=jnp.float32), 'src': jax.random.randint(ks[10], (E,), 0, N, dtype=jnp.int64 if jax.config.jax_enable_x64 else jnp.int32), 'dst': jax.random.randint(ks[11], (E,), 0, N, dtype=jnp.int64 if jax.config.jax_enable_x64 else jnp.int32)}
        return inp
    _L0_gnn_all = _L0_gnn_setup()
    _L0_gnn_in = {k: v for k, v in _L0_gnn_all.items() if k in ('W_low', 'W_high', 'W_mlp', 'av_low', 'av_high', 'av_mlp', 'att_vec')}
    del _L0_gnn_all

    def _L1_gnn_setup():
        import jax, jax.numpy as jnp
        import numpy as np
        N_NODES = 12500
        N_EDGES = 400000
        EDGE_OUT = 32
        HID = 128
        NODE_OUT = 64
        N_GRAPHS = 16
        key = jax.random.key(seed)
        ks = jax.random.split(key, 9)
        x = jax.random.normal(ks[0], (N_NODES, 64), dtype=jnp.float32)
        edge_index = jax.random.randint(ks[1], (2, N_EDGES), 0, N_NODES, dtype=jnp.int64)
        edge_attr = jax.random.normal(ks[2], (N_EDGES, EDGE_OUT), dtype=jnp.float32)
        u = jax.random.normal(ks[3], (N_GRAPHS, 1), dtype=jnp.float32)
        batch = jnp.sort(jax.random.randint(ks[4], (N_NODES,), 0, N_GRAPHS, dtype=jnp.int64))
        d_in = 3 * EDGE_OUT + 1
        W1 = jax.random.normal(ks[5], (d_in, HID), dtype=jnp.float32) / np.sqrt(d_in)
        b1 = jnp.zeros((HID,), dtype=jnp.float32)
        W2 = jax.random.normal(ks[6], (HID, NODE_OUT), dtype=jnp.float32) / np.sqrt(HID)
        b2 = jnp.zeros((NODE_OUT,), dtype=jnp.float32)
        return {'x': x, 'edge_index': edge_index, 'edge_attr': edge_attr, 'u': u, 'batch': batch, 'W1': W1, 'b1': b1, 'W2': W2, 'b2': b2}
    _L1_gnn_all = _L1_gnn_setup()
    _L1_gnn_in = {k: v for k, v in _L1_gnn_all.items() if k in ('u', 'W1', 'b1', 'W2', 'b2')}
    del _L1_gnn_all

    def _L2_gnn_setup():
        import jax, jax.numpy as jnp
        import numpy as np
        N, E, D, K, PDIM = (12500, 200000, 64, 4, 2)
        EPS = 1e-15
        key = jax.random.key(seed)
        k1, k2, k3, k4, k5, k6 = jax.random.split(key, 6)
        x = jax.random.normal(k1, (N, D), dtype=jnp.float32)
        edge_index = jax.random.randint(k2, (2, E), 0, N, dtype=jnp.int64)
        g = jax.random.normal(k3, (D, K * D), dtype=jnp.float32) / np.sqrt(D)
        mu = jax.random.normal(k4, (K, PDIM), dtype=jnp.float32)
        sigma = jax.random.uniform(k5, (K, PDIM), dtype=jnp.float32, minval=0.5, maxval=1.5)
        root = jax.random.normal(k6, (D, D), dtype=jnp.float32) / np.sqrt(D)
        bias = jnp.zeros((D,), dtype=jnp.float32)
        return {'x': x, 'edge_index': edge_index, 'g': g, 'mu': mu, 'sigma': sigma, 'root': root, 'bias': bias}
    _L2_gnn_all = _L2_gnn_setup()
    _L2_gnn_in = {k: v for k, v in _L2_gnn_all.items() if k in ('g', 'mu', 'sigma', 'root', 'bias')}
    del _L2_gnn_all

    def _L3_gnn_setup():
        import jax, jax.numpy as jnp
        import numpy as np
        N_NODES = 12500
        N_EDGES = 125000
        NODE_DIM = 64
        EDGE_DIM = 32
        HIDDEN = 64

        def _unif(key, shape, fan_in):
            bound = 1.0 / np.sqrt(fan_in)
            return jax.random.uniform(key, shape, jnp.float32, -bound, bound)
        key = jax.random.key(seed)
        ks = jax.random.split(key, 11)
        node_features = jax.random.normal(ks[0], (N_NODES, NODE_DIM), jnp.float32)
        edge_index = jax.random.randint(ks[1], (2, N_EDGES), 0, N_NODES, dtype=jnp.int64)
        edge_features = jax.random.normal(ks[2], (N_EDGES, EDGE_DIM), jnp.float32)
        in_dim = 2 * NODE_DIM + EDGE_DIM
        W1 = _unif(ks[3], (HIDDEN, in_dim), in_dim)
        b1 = _unif(ks[4], (HIDDEN,), in_dim)
        W2 = _unif(ks[5], (HIDDEN, HIDDEN), HIDDEN)
        b2 = _unif(ks[6], (HIDDEN,), HIDDEN)
        w_ih = _unif(ks[7], (3 * NODE_DIM, HIDDEN), NODE_DIM)
        w_hh = _unif(ks[8], (3 * NODE_DIM, NODE_DIM), NODE_DIM)
        b_ih = _unif(ks[9], (3 * NODE_DIM,), NODE_DIM)
        b_hh = _unif(ks[10], (3 * NODE_DIM,), NODE_DIM)
        return {'node_features': node_features, 'edge_index': edge_index, 'edge_features': edge_features, 'W1': W1, 'b1': b1, 'W2': W2, 'b2': b2, 'w_ih': w_ih, 'w_hh': w_hh, 'b_ih': b_ih, 'b_hh': b_hh}
    _L3_gnn_all = _L3_gnn_setup()
    _L3_gnn_in = {k: v for k, v in _L3_gnn_all.items() if k in ('W1', 'b1', 'W2', 'b2', 'w_ih', 'w_hh', 'b_ih', 'b_hh')}
    del _L3_gnn_all
    return {'x': x, 'src': src, 'dst': dst, 'edge_attr_32': edge_attr_32, 'edge_weight': edge_weight, 'edge_weight_n2': edge_weight_n2, 'L0_gnn_W_low': _L0_gnn_in['W_low'], 'L0_gnn_W_high': _L0_gnn_in['W_high'], 'L0_gnn_W_mlp': _L0_gnn_in['W_mlp'], 'L0_gnn_av_low': _L0_gnn_in['av_low'], 'L0_gnn_av_high': _L0_gnn_in['av_high'], 'L0_gnn_av_mlp': _L0_gnn_in['av_mlp'], 'L0_gnn_att_vec': _L0_gnn_in['att_vec'], 'L1_gnn_u': _L1_gnn_in['u'], 'L1_gnn_W1': _L1_gnn_in['W1'], 'L1_gnn_b1': _L1_gnn_in['b1'], 'L1_gnn_W2': _L1_gnn_in['W2'], 'L1_gnn_b2': _L1_gnn_in['b2'], 'L2_gnn_g': _L2_gnn_in['g'], 'L2_gnn_mu': _L2_gnn_in['mu'], 'L2_gnn_sigma': _L2_gnn_in['sigma'], 'L2_gnn_root': _L2_gnn_in['root'], 'L2_gnn_bias': _L2_gnn_in['bias'], 'L3_gnn_W1': _L3_gnn_in['W1'], 'L3_gnn_b1': _L3_gnn_in['b1'], 'L3_gnn_W2': _L3_gnn_in['W2'], 'L3_gnn_b2': _L3_gnn_in['b2'], 'L3_gnn_w_ih': _L3_gnn_in['w_ih'], 'L3_gnn_w_hh': _L3_gnn_in['w_hh'], 'L3_gnn_b_ih': _L3_gnn_in['b_ih'], 'L3_gnn_b_hh': _L3_gnn_in['b_hh']}

def reference(x, src, dst, edge_attr_32, edge_weight, edge_weight_n2, L0_gnn_W_low, L0_gnn_W_high, L0_gnn_W_mlp, L0_gnn_av_low, L0_gnn_av_high, L0_gnn_av_mlp, L0_gnn_att_vec, L1_gnn_u, L1_gnn_W1, L1_gnn_b1, L1_gnn_W2, L1_gnn_b2, L2_gnn_g, L2_gnn_mu, L2_gnn_sigma, L2_gnn_root, L2_gnn_bias, L3_gnn_W1, L3_gnn_b1, L3_gnn_W2, L3_gnn_b2, L3_gnn_w_ih, L3_gnn_w_hh, L3_gnn_b_ih, L3_gnn_b_hh):
    import jax
    import jax.numpy as jnp

    def _L0_gnn_ref(x, w_low, w_high, W_low, W_high, W_mlp, av_low, av_high, av_mlp, att_vec, src, dst):
        import jax, jax.numpy as jnp
        import numpy as np
        N = 12500
        E = 200000
        D_IN = 64
        D_OUT = 64

        def _spmm(w, src, dst, h, n):
            return jax.ops.segment_sum(w[:, None] * h[src], dst, num_segments=n)
        n = x.shape[0]
        h_low = jax.nn.relu(_spmm(w_low, src, dst, x @ W_low, n))
        h_high = jax.nn.relu(_spmm(w_high, src, dst, x @ W_high, n))
        h_mlp = jax.nn.relu(x @ W_mlp)
        feats = jnp.concatenate([h_low @ av_low, h_high @ av_high, h_mlp @ av_mlp], axis=1)
        logits = jax.nn.sigmoid(feats) @ att_vec / 3.0
        att = jax.nn.softmax(logits, axis=1)
        out = 3.0 * (att[:, 0:1] * h_low + att[:, 1:2] * h_high + att[:, 2:3] * h_mlp)
        return out

    def _L1_gnn_ref(x, edge_index, edge_attr, u, batch, W1, b1, W2, b2):
        import jax, jax.numpy as jnp
        import numpy as np
        N_NODES = 12500
        N_EDGES = 400000
        EDGE_OUT = 32
        HID = 128
        NODE_OUT = 64
        N_GRAPHS = 16
        N = x.shape[0]
        row = edge_index[0]
        seg_sum = jax.ops.segment_sum(edge_attr, row, num_segments=N)
        seg_max = jax.ops.segment_max(edge_attr, row, num_segments=N)
        cnt = jax.ops.segment_sum(jnp.ones((edge_attr.shape[0], 1), edge_attr.dtype), row, num_segments=N)
        seg_mean = seg_sum / jnp.maximum(cnt, 1.0)
        seg_max = jnp.where(cnt > 0, seg_max, 0.0)
        h = jnp.concatenate([seg_sum, seg_max, seg_mean, u[batch]], axis=1)
        h = jax.nn.relu(h @ W1 + b1)
        return h @ W2 + b2

    def _L2_gnn_ref(x, edge_index, g, mu, sigma, root, bias):
        import jax, jax.numpy as jnp
        import numpy as np
        N, E, D, K, PDIM = (12500, 200000, 64, 4, 2)
        EPS = 1e-15
        src, dst = (edge_index[0], edge_index[1])
        n = x.shape[0]
        deg = jax.ops.segment_sum(jnp.ones((src.shape[0],), x.dtype), dst, num_segments=n)
        deg = jnp.maximum(deg, 1.0)
        inv_sqrt_deg = jax.lax.rsqrt(deg)
        pseudo = jnp.stack([inv_sqrt_deg[src], inv_sqrt_deg[dst]], axis=-1)
        diff = pseudo[:, None, :] - mu[None, :, :]
        gw = jnp.exp(jnp.sum(-0.5 * diff * diff / (EPS + sigma * sigma)[None], axis=-1))
        xt = (x @ g).reshape(n, K, -1)
        agg = jnp.zeros((n, xt.shape[-1]), x.dtype)
        for k in range(K):
            msg = gw[:, k, None] * xt[src, k]
            agg = agg + jax.ops.segment_sum(msg, dst, num_segments=n)
        agg = agg / deg[:, None]
        conv = agg + x @ root + bias
        return x + jax.nn.relu(conv)

    def _L3_gnn_ref(node_features, edge_index, edge_features, W1, b1, W2, b2, w_ih, w_hh, b_ih, b_hh):
        import jax, jax.numpy as jnp
        import numpy as np
        N_NODES = 12500
        N_EDGES = 125000
        NODE_DIM = 64
        EDGE_DIM = 32
        HIDDEN = 64

        def _unif(key, shape, fan_in):
            bound = 1.0 / np.sqrt(fan_in)
            return jax.random.uniform(key, shape, jnp.float32, -bound, bound)
        src, dst = (edge_index[0], edge_index[1])
        x = jnp.concatenate([node_features[src], node_features[dst], edge_features], axis=-1)
        h = jax.nn.relu(x @ W1.T + b1)
        messages = h @ W2.T + b2
        agg = jax.ops.segment_sum(messages, dst, num_segments=node_features.shape[0])
        gi = agg @ w_ih.T + b_ih
        gh = node_features @ w_hh.T + b_hh
        i_r, i_z, i_n = jnp.split(gi, 3, axis=-1)
        h_r, h_z, h_n = jnp.split(gh, 3, axis=-1)
        r = jax.nn.sigmoid(i_r + h_r)
        z = jax.nn.sigmoid(i_z + h_z)
        n = jnp.tanh(i_n + r * h_n)
        return (1.0 - z) * n + z * node_features
    edge_index = jnp.stack([src, dst])
    batch0 = jnp.zeros((6250,), jnp.int32)
    x = _layernorm(x + _L0_gnn_ref(x, edge_weight, edge_weight_n2, L0_gnn_W_low, L0_gnn_W_high, L0_gnn_W_mlp, L0_gnn_av_low, L0_gnn_av_high, L0_gnn_av_mlp, L0_gnn_att_vec, src, dst), axis=-1)
    x = _layernorm(x + _L1_gnn_ref(x, edge_index, edge_attr_32, L1_gnn_u, batch0, L1_gnn_W1, L1_gnn_b1, L1_gnn_W2, L1_gnn_b2), axis=-1)
    x = _layernorm(x + _L2_gnn_ref(x, edge_index, L2_gnn_g, L2_gnn_mu, L2_gnn_sigma, L2_gnn_root, L2_gnn_bias), axis=-1)
    x = _layernorm(x + _L3_gnn_ref(x, edge_index, edge_attr_32, L3_gnn_W1, L3_gnn_b1, L3_gnn_W2, L3_gnn_b2, L3_gnn_w_ih, L3_gnn_w_hh, L3_gnn_b_ih, L3_gnn_b_hh), axis=-1)
    return x

_drawn_inputs = setup_inputs


def setup_inputs(seed=0):
    import zlib

    import numpy as np

    out = dict(_drawn_inputs(seed))
    spreads = {'L1_gnn_b1': (0.0, 0.283), 'L1_gnn_b2': (0.0, 0.1), 'L2_gnn_bias': (0.0, 0.1)}
    factors = {'L0_gnn_av_low': 4.058, 'L0_gnn_av_mlp': 3.999, 'L3_gnn_b_ih': 4.577, 'L3_gnn_b_hh': 5.305}
    for name, (base, spread) in spreads.items():
        noise = np.random.default_rng([zlib.crc32(name.encode()), seed]).standard_normal(out[name].shape)
        drawn = base * np.exp(spread * noise) if base else spread * noise
        out[name] = jnp.asarray(drawn.astype(out[name].dtype))
    for name, factor in factors.items():
        out[name] = (out[name] * factor).astype(out[name].dtype)
    return out
```

```python
import concourse.bass as bass
from concourse import mybir
from contextlib import ExitStack


P = 128
CH = 16
GE = P * CH
D = 64
F = 32
RW = F + 1
HID = 128
W = 128
TB = 7
BIG = 3.0e38
EPS = 1e-5

fp32 = mybir.dt.float32
bf16 = mybir.dt.bfloat16
i32 = mybir.dt.int32
ALU = mybir.AluOpType
ACT = mybir.ActivationFunctionType
AX = mybir.AxisListType.X


class Names:
    pass


def sizes(n, e):
    groups = -(-e // GE)
    groups += 1 - groups % 2
    tiles = -(-(n + 1) // P)
    tiles = -(-tiles // TB) * TB
    z = Names()
    z.n, z.e, z.G, z.EP = n, e, groups, groups * GE
    z.NT, z.NP, z.NC, z.NB = tiles, tiles * P, tiles * P + W, tiles // TB
    return z


def at(g, size=1):
    return bass.ds(g * size, size)


def wait(eng, sem, value):
    if isinstance(value, int) and value <= 0:
        return
    eng.wait_ge(sem, value)


def over_groups(eng, groups, body):
    first = min(3, groups)
    for g in range(first):
        body(g, g % 2)
    if groups > first:
        with eng.Fori(0, (groups - first) // 2) as i:
            body(i * 2 + first, first % 2)
            body(i * 2 + first + 1, (first + 1) % 2)


def over_blocks(eng, blocks, body):
    if blocks > 1:
        with eng.Fori(0, blocks - 1) as b:
            body(b, True)
    body(blocks - 1, False)


def make(nc, ctx):
    def sb(name, shape, dt=fp32):
        return ctx.enter_context(nc.sbuf_tensor(name, shape, dt))

    def ps(name, shape, dt=fp32):
        return ctx.enter_context(nc.psum_tensor(name, shape, dt))

    def sem(name):
        return ctx.enter_context(nc.semaphore(name))

    return sb, ps, sem


def setup(nc, z, k, a):
    with ExitStack() as ctx:
        sb, ps, sem = make(nc, ctx)
        dst_g = sb("dst_g", [z.G, GE], i32)
        src_g = sb("src_g", [z.G, GE], i32)
        hi_g = sb("hi_g", [z.G, GE], i32)
        lo_g = sb("lo_g", [z.G, GE], i32)
        hi_b = sb("hi_b", [z.G, GE], bf16)
        lo_b = sb("lo_b", [z.G, GE], bf16)
        dstf_g = sb("dstf_g", [z.G, GE])
        span = sb("span", [z.G, 4])
        span_i = sb("span_i", [z.G, 2], i32)
        spans = sb("spans", [P, z.G, 2])
        incl = sb("windows_incl", [1, z.G])
        ones_row = sb("ones_row", [1, z.G])
        pc_i = sb("pc_i", [P, z.G * CH], i32)
        pc_j = sb("pc_j", [P, z.G * CH], i32)
        it = sb("iota_i", [P, P], i32)
        itp = sb("iota_pi", [P, 1], i32)
        loads = sem("setup_loads")
        pc_src = sem("setup_src")
        pc_dst = sem("setup_dst")
        span_out = sem("span_out")
        span_in = sem("span_in")
        parts = sem("hi_lo_out")
        spans_ready = sem("spans_ready")
        halves_ready = sem("halves_ready")
        iotas = sem("iotas")
        ones_set = sem("ones_set")
        src_used = sem("src_used")
        with nc.Block() as block:

            @block.sync
            def _(sp):
                sp.dma_start(dst_g[:, :], a["dst"].rearrange("(g e) -> g e", g=z.G)).then_inc(loads, 16)
                sp.dma_start(src_g[:, :], a["src"].rearrange("(g e) -> g e", g=z.G)).then_inc(loads, 16)
                sp.dma_start(pc_i[:, :].rearrange("p (g c) -> p g c", c=CH),
                             a["src"].rearrange("(g p c) -> p g c", p=P, c=CH)).then_inc(pc_src, 16)
                sp.dma_start(pc_j[:, :].rearrange("p (g c) -> p g c", c=CH),
                             a["dst"].rearrange("(g p c) -> p g c", p=P, c=CH)).then_inc(pc_dst, 16)
                sp.wait_ge(spans_ready, 1)
                sp.dma_start(a["span_d"], span[:, 0:2]).then_inc(span_out, 16)
                sp.wait_ge(span_out, 16)
                sp.dma_start(spans[:, :, :].rearrange("p g s -> p (g s)"),
                             a["span_d"].rearrange("(a g) s -> a (g s)", a=1).to_broadcast([P, 2 * z.G])).then_inc(span_in, 16)
                sp.wait_ge(halves_ready, 2)
                sp.dma_start(a["hilo_d"][0].rearrange("(g e) -> g e", g=z.G), hi_b[:, :]).then_inc(parts, 16)
                sp.dma_start(a["hilo_d"][1].rearrange("(g e) -> g e", g=z.G), lo_b[:, :]).then_inc(parts, 16)
                sp.wait_ge(parts, 32)

            @block.gpsimd
            def _(pool):
                pool.iota(it[:, :], pattern=[[1, P]], base=0, channel_multiplier=0).then_inc(iotas, 1)
                pool.iota(itp[:, :], pattern=[[0, 1]], base=0, channel_multiplier=1).then_inc(iotas, 1)
                pool.memset(k.ones[:, :], 1.0).then_inc(ones_set, 1)
                pool.wait_ge(ones_set, 1)
                pool.affine_select(out=k.ident[:, :], in_=k.ones[:, :], compare_op=ALU.is_equal, fill=0.0,
                                   base=0, pattern=[[-1, P]], channel_multiplier=1)
                pool.affine_select(out=k.before[:, :], in_=k.ones[:, :], compare_op=ALU.is_gt, fill=0.0,
                                   base=0, pattern=[[-1, P]], channel_multiplier=1)
                pool.affine_select(out=k.after[:, :], in_=k.ones[:, :], compare_op=ALU.is_gt, fill=0.0,
                                   base=0, pattern=[[1, P]], channel_multiplier=-1)
                pool.affine_select(out=k.pick[:, 0, :], in_=k.ones[0:2, :], compare_op=ALU.is_gt, fill=float(P),
                                   base=0, pattern=[[0, P]], channel_multiplier=1)
                pool.affine_select(out=k.pick[:, 1, :], in_=k.ones[0:2, :], compare_op=ALU.is_gt, fill=0.0,
                                   base=0, pattern=[[0, P]], channel_multiplier=1)
                pool.drain()

            @block.vector
            def _(dve):
                v = nc.vector
                v.memset(k.acc0[:, :], 0.0)
                v.memset(ones_row[:, :], 1.0)
                dve.wait_ge(iotas, 2)
                v.tensor_copy(k.iota[:, :], it[:, :])
                v.tensor_copy(k.iota_p[:, :], itp[:, :])
                dve.wait_ge(loads, 32)
                v.tensor_copy(dstf_g[:, :], dst_g[:, :])
                dve.drain()
                v.tensor_reduce(span[:, 0:1], dstf_g[:, :], AX, ALU.min)
                v.tensor_reduce(span[:, 2:3], dstf_g[:, :], AX, ALU.max)
                dve.drain()
                v.tensor_tensor(span_i[:, 0:1], span[:, 2:3], span[:, 0:1], ALU.subtract)
                dve.drain()
                v.tensor_scalar(span_i[:, 1:2], span_i[:, 0:1], 7, None, ALU.logical_shift_right)
                dve.drain()
                v.tensor_scalar(span[:, 1:2], span_i[:, 1:2], 1.0, None, ALU.add).then_inc(spans_ready, 1)
                v.tensor_scalar(hi_g[:, :], src_g[:, :], 7, None, ALU.logical_shift_right)
                v.tensor_scalar(lo_g[:, :], src_g[:, :], P - 1, None, ALU.bitwise_and)
                dve.drain()
                v.tensor_copy(hi_b[:, :], hi_g[:, :]).then_inc(halves_ready, 1)
                v.tensor_copy(lo_b[:, :], lo_g[:, :]).then_inc(halves_ready, 1)
                dve.wait_ge(pc_src, 16)
                v.tensor_copy(k.src[:, :], pc_i[:, :])
                dve.wait_ge(pc_dst, 16)
                v.tensor_copy(k.dst[:, :], pc_j[:, :])
                dve.wait_ge(span_in, 16)
                v.tensor_tensor_scan(incl[:, :], ones_row[:, :], spans[0:1, :, 1], 0.0, ALU.mult, ALU.add)
                dve.drain()
                v.tensor_copy(k.table[:, :, 0], spans[0:1, :, 0])
                v.tensor_copy(k.table[:, :, 1], spans[0:1, :, 1])
                v.tensor_tensor(k.table[:, :, 2], incl[:, :], spans[0:1, :, 1], ALU.subtract)
                v.tensor_copy(k.table[:, :, 3], incl[:, :])
                v.tensor_tensor(k.rel[:, :].rearrange("p (g c) -> p g c", c=CH),
                                k.dst[:, :].rearrange("p (g c) -> p g c", c=CH),
                                spans[:, :, 0:1].to_broadcast([P, z.G, CH]), ALU.subtract)
                for full, hi, lo in ((k.src, k.src_hi, k.src_lo), (k.dst, k.dst_hi, k.dst_lo)):
                    raw = pc_i if full is k.src else pc_j
                    dve.drain()
                    v.tensor_scalar(raw[:, :], raw[:, :], 7, None, ALU.logical_shift_right)
                    dve.drain()
                    v.tensor_copy(hi[:, :], raw[:, :])
                    dve.drain()
                    v.scalar_tensor_tensor(out=lo[:, :], in0=hi[:, :], scalar=-float(P), in1=full[:, :],
                                           op0=ALU.mult, op1=ALU.add)
                dve.drain()


def layer0_edges(nc, z, k, a):
    with ExitStack() as ctx:
        sb, ps, sem = make(nc, ctx)
        idx = [sb(f"idx{b}", [P, CH], i32) for b in range(2)]
        rows = [sb(f"rows{b}", [P, CH, D]) for b in range(2)]
        w_lo = sb("w_lo", [P, z.G * CH])
        w_hi = sb("w_hi", [P, z.G * CH])
        val = [sb(f"val{b}", [P, CH, 2 * D]) for b in range(2)]
        hot_lo = [sb(f"hot_lo{b}", [P, 2, CH, P], bf16) for b in range(2)]
        hot_hi = [sb(f"hot_hi{b}", [P, 2, CH, z.NT], bf16) for b in range(2)]
        onehot = sb("onehot", [P, CH, W])
        cur = sb("cur", [P, CH])
        zero = sb("zero", [P, P], bf16)
        counts = ps("counts", [P, 2, 512])
        win = ps("win", [P, W])
        idx_in = [sem(f"idx_in{b}") for b in range(2)]
        weights_in = sem("weights_in")
        rows_in = [sem(f"rows_in{b}") for b in range(2)]
        val_ready = sem("val_ready")
        hot_ready = sem("hot_ready")
        onehot_ready = sem("onehot_ready")
        win_ready = sem("win_ready")
        group_done = sem("group_done")
        counts_done = sem("counts_done")
        zero_set = sem("zero_set")
        cnt_saved = sem("cnt_saved")
        iv = a["src"].rearrange("(g p c) -> g p c", p=P, c=CH)
        with nc.Block() as block:

            @block.sync
            def _(sp):
                wv = lambda w: w.rearrange("(g p c) -> p g c", p=P, c=CH)
                sp.dma_start(w_lo[:, :].rearrange("p (g c) -> p g c", c=CH), wv(a["w_low"])).then_inc(weights_in, 16)
                sp.dma_start(w_hi[:, :].rearrange("p (g c) -> p g c", c=CH), wv(a["w_high"])).then_inc(weights_in, 16)

                def group(g, b):
                    if not (isinstance(g, int) and g < 2):
                        sp.wait_ge(rows_in[b], (g - b) * (CH * 8))
                    sp.sem_inc(k.sync_groups, 1)
                    sp.dma_start(idx[b][:, :], iv[at(g)].rearrange("g p c -> (g p) c")).then_inc(idx_in[b], 16)
                over_groups(sp, z.G, group)

            @block.gpsimd
            def _(pool):
                def group(g, b):
                    pool.wait_ge(idx_in[b], (g - b) * 8 + 16)
                    wait(pool, val_ready, (g - 1) * (2 * CH))
                    pool.sem_inc(k.pool_groups, 1)
                    for c in range(CH):
                        pool.indirect_dma_start(rows[b][:, c, :], None, a["x"][:, :],
                                                bass.IndirectOffsetOnAxis(ap=idx[b][:, c:c + 1], axis=0)
                                                ).then_inc(rows_in[b], 16)
                over_groups(pool, z.G, group)

            @block.vector
            def _(dve):
                v = nc.vector
                v.memset(zero[:, :], 0.0).then_inc(zero_set, 1)

                def group(g, b):
                    wait(dve, counts_done, g - 1)
                    for s, (lo, hi) in enumerate(((k.src_lo, k.src_hi), (k.dst_lo, k.dst_hi))):
                        v.tensor_tensor(hot_lo[b][:, s], k.iota[:, :].unsqueeze(1).to_broadcast([P, CH, P]),
                                        lo[:, at(g, CH)].unsqueeze(2).to_broadcast([P, CH, P]),
                                        ALU.is_equal).then_inc(hot_ready, 1)
                        v.tensor_tensor(hot_hi[b][:, s], k.iota[:, 0:z.NT].unsqueeze(1).to_broadcast([P, CH, z.NT]),
                                        hi[:, at(g, CH)].unsqueeze(2).to_broadcast([P, CH, z.NT]),
                                        ALU.is_equal).then_inc(hot_ready, 1)
                    windows_vector(nc, dve, k, g, onehot, cur, [(k.acc0, win[:, :])], onehot_ready, win_ready, group_done)
                over_groups(dve, z.G, group)
                dve.wait_ge(group_done, z.G)
                dve.wait_ge(counts_done, z.G + 1)
                v.tensor_copy(k.cnt_src[:, :], counts[:, 0, 0:z.NT]).then_inc(cnt_saved, 1)
                v.tensor_copy(k.cnt_dst[:, :], counts[:, 1, 0:z.NT]).then_inc(cnt_saved, 1)
                dve.wait_ge(cnt_saved, 2)

            @block.scalar
            def _(act):
                act.wait_ge(weights_in, 32)

                def group(g, b):
                    wait(act, group_done, g - 1)
                    act.wait_ge(rows_in[b], (g - b) * (CH * 8) + CH * 16)
                    for c in range(CH):
                        for s, w in enumerate((w_lo, w_hi)):
                            nc.scalar.activation(val[b][:, c, s * D:(s + 1) * D], rows[b][:, c, :], ACT.Copy,
                                                 scale=w[:, bass.ds(g * CH + c, 1)]).then_inc(val_ready, 1)
                over_groups(act, z.G, group)

            @block.tensor
            def _(pe):
                pe.wait_ge(zero_set, 1)
                for s in range(2):
                    nc.tensor.matmul(counts[:, s, 0:z.NT], zero[:, :], zero[:, 0:z.NT], start=True, stop=False)

                def group(g, b):
                    pe.wait_ge(hot_ready, g * 4 + 4)
                    for s in range(2):
                        for c in range(CH):
                            last = nc.tensor.matmul(counts[:, s, 0:z.NT], hot_lo[b][:, s, c, :],
                                                    hot_hi[b][:, s, c, :], start=False, stop=False)
                    last.then_inc(counts_done, 1)
                    def window():
                        for c in range(CH):
                            last = nc.tensor.matmul(win[:, :], val[b][:, c, :], onehot[:, c, :],
                                                    start=(c == 0), stop=(c == CH - 1))
                        return last
                    windows_tensor(pe, k, g, window, onehot_ready, win_ready, val_ready, g * (2 * CH) + 2 * CH)
                over_groups(pe, z.G, group)
                for s in range(2):
                    last = nc.tensor.matmul(counts[:, s, 0:z.NT], zero[:, :], zero[:, 0:z.NT], start=False, stop=True)
                last.then_inc(counts_done, 1)


def table_row(eng, k, g):
    row = k.table[0:1, at(g), :].rearrange("a g s -> a (g s)")
    base = eng.value_load(row[:, 0:1], min_val=0, max_val=k.table_limits[0])
    count = eng.value_load(row[:, 1:2], min_val=1, max_val=k.table_limits[1])
    before = eng.value_load(row[:, 2:3], min_val=0, max_val=k.table_limits[2])
    return base, count, before


def windows_vector(nc, dve, k, g, onehot, cur, sums, onehot_ready, win_ready, group_done=None):
    v = nc.vector
    base, count, before = table_row(dve, k, g)
    v.tensor_copy(cur[:, :], k.rel[:, at(g, CH)])
    with dve.Fori(0, count) as w:
        dve.drain()
        v.tensor_tensor(onehot[:, :, :], k.iota[:, :].unsqueeze(1).to_broadcast([P, CH, W]),
                        cur[:, :].unsqueeze(2).to_broadcast([P, CH, W]), ALU.is_equal).then_inc(onehot_ready, 1)
        dve.drain()
        v.tensor_scalar(cur[:, :], cur[:, :], -float(W), None, ALU.add)
        dve.wait_ge(win_ready, before + w + 1)
        col = (base + w * W).with_bounds(min_val=0, max_val=k.table_limits[0])
        for acc, win in sums:
            v.tensor_tensor(acc[:, bass.ds(col, W)], win, acc[:, bass.ds(col, W)], ALU.add)
    last = dve.drain()
    if group_done is not None:
        last.then_inc(group_done, 1)


def windows_tensor(pe, k, g, window, onehot_ready, win_ready, operands, value):
    base, count, before = table_row(pe, k, g)
    with pe.Fori(0, count) as w:
        pe.wait_ge(operands, value)
        pe.wait_ge(onehot_ready, before + w + 1)
        window().then_inc(win_ready, 1)


def norm_vector(nc, dve, k, y, s, b, eps_in, eps_out, done):
    v = nc.vector
    flat = k.x[:, bass.ds(b * (TB * D), TB * D)].rearrange("p (t d) -> p t d", d=D)
    mean = s[:, 0:TB]
    var = s[:, TB:2 * TB]
    dve.drain()
    v.tensor_reduce(mean, y[:, :, :], AX, ALU.add)
    dve.drain()
    v.tensor_scalar(mean, mean, 1.0 / D, None, ALU.mult)
    dve.drain()
    v.tensor_tensor(y[:, :, :], y[:, :, :], mean.unsqueeze(2).to_broadcast([P, TB, D]), ALU.subtract)
    dve.drain()
    v.tensor_tensor(k.sq[:, :, :], y[:, :, :], y[:, :, :], ALU.mult)
    dve.drain()
    v.tensor_reduce(var, k.sq[:, :, :], AX, ALU.add)
    dve.drain()
    v.tensor_scalar(var, var, 1.0 / D, EPS, ALU.mult, ALU.add).then_inc(eps_in, 1)
    dve.wait_ge(eps_out, b + 1)
    v.reciprocal(mean, s[:, 2 * TB:3 * TB])
    dve.drain()
    v.tensor_tensor(flat, y[:, :, :], mean.unsqueeze(2).to_broadcast([P, TB, D]), ALU.mult).then_inc(done, 1)
    dve.drain()


def norm_scalar(nc, act, s, b, eps_in, eps_out):
    act.wait_ge(eps_in, b + 1)
    nc.scalar.activation(s[:, 2 * TB:3 * TB], s[:, TB:2 * TB], ACT.Sqrt).then_inc(eps_out, 1)


def layer0_nodes(nc, z, k, a):
    with ExitStack() as ctx:
        sb, ps, sem = make(nc, ctx)
        w_low = sb("W_low", [P, D])
        w_high = sb("W_high", [P, D])
        w_mlp = sb("W_mlp", [D, D])
        av = sb("av", [P, 3 * D])
        att_vec = sb("att_vec", [P, 9])
        xb = sb("xb", [P, TB, D])
        xt = sb("xt", [D, TB * P])
        agg = sb("agg", [P, TB * P])
        h = sb("h", [P, TB, 3 * D])
        hp = sb("hp", [P, TB, 3 * D])
        f3 = sb("f3", [P, TB, 3])
        g3 = sb("g3", [P, TB, 3])
        l9 = sb("l9", [P, TB, 9])
        m1 = sb("m1", [P, TB])
        y = sb("y", [P, TB, D])
        s = sb("s", [P, 3 * TB])
        pb = ps("branches", [P, 3, 512])
        consts_in, x_in, staged, mm, relu, feats, sig, logit, expd, eps_in, eps_out, done = (
            sem(n) for n in ("consts_in", "x_in", "staged", "branches_ready", "relu_ready", "feats_ready",
                             "sigmoid_ready", "logits_ready", "exp_ready", "var_ready", "std_ready", "x1_ready"))
        xt_in = sem("xt_in")
        blocks = sem("blocks_through")
        xv = a["x"].rearrange("(b t p) d -> b p t d", p=P, t=TB)
        with nc.Block() as block:

            @block.sync
            def _(sp):
                sp.dma_start(w_low[0:D, :], a["L0_gnn_W_low"]).then_inc(consts_in, 16)
                sp.dma_start(w_high[D:P, :], a["L0_gnn_W_high"]).then_inc(consts_in, 16)
                sp.dma_start(w_mlp[:, :], a["L0_gnn_W_mlp"]).then_inc(consts_in, 16)
                for n, w in enumerate((a["L0_gnn_av_low"], a["L0_gnn_av_high"], a["L0_gnn_av_mlp"])):
                    sp.dma_start(av[:, n * D:(n + 1) * D], w.rearrange("d a -> a d").to_broadcast([P, D])).then_inc(consts_in, 16)
                sp.dma_start(att_vec[:, :], a["L0_gnn_att_vec"].rearrange("(a i) j -> a (i j)", a=1).to_broadcast([P, 9])).then_inc(consts_in, 16)

                def load_turned(b):
                    sp.dma_start(xt[:, :], a["xT"][:, at(b, TB * P)]).then_inc(xt_in, 16)

                def load(b):
                    sp.dma_start(xb[:, :, :], xv[at(b)].rearrange("b p t d -> (b p) t d")).then_inc(x_in, 16)
                load_turned(0)
                load(0)
                with sp.Fori(0, z.NB - 1) as b:
                    sp.wait_ge(mm, b + 1)
                    sp.sem_inc(blocks, 1)
                    load_turned(b + 1)
                    sp.wait_ge(done, b + 1)
                    sp.sem_inc(blocks, 1)
                    load(b + 1)
                sp.wait_ge(blocks, 2 * (z.NB - 1))

            @block.scalar
            def _(act):
                sc = nc.scalar

                def stage(b):
                    sc.activation(agg[:, :], k.acc0[:, at(b, TB * P)], ACT.Copy).then_inc(staged, 1)

                def block_(b, more):
                    act.wait_ge(mm, b + 1)
                    sc.activation(h[:, :, :].rearrange("p t (j d) -> p j t d", d=D),
                                  pb[:, :, 0:TB * D].rearrange("p j (t d) -> p j t d", d=D), ACT.Relu).then_inc(relu, 1)
                    if more:
                        stage(b + 1)
                    act.wait_ge(feats, b + 1)
                    sc.activation(g3[:, :, :], f3[:, :, :], ACT.Sigmoid).then_inc(sig, 1)
                    act.wait_ge(logit, b + 1)
                    sc.activation(g3[:, :, :], f3[:, :, :], ACT.Exp, scale=1.0 / 3.0).then_inc(expd, 1)
                    norm_scalar(nc, act, s, b, eps_in, eps_out)
                stage(0)
                over_blocks(act, z.NB, block_)

            @block.tensor
            def _(pe):
                pe.wait_ge(consts_in, 16 * 7)
                with pe.Fori(0, z.NB) as b:
                    pe.wait_ge(staged, b + 1)
                    pe.wait_ge(xt_in, b * 16 + 16)
                    for t in range(TB):
                        col = slice(t * P, (t + 1) * P)
                        o = slice(t * D, (t + 1) * D)
                        nc.tensor.matmul(pb[:, 0, o], agg[0:D, col], w_low[0:D, :], start=True, stop=True)
                        nc.tensor.matmul(pb[:, 1, o], agg[D:P, col], w_high[D:P, :], start=True, stop=True)
                        last = nc.tensor.matmul(pb[:, 2, o], xt[:, col], w_mlp[:, :], start=True, stop=True)
                    last.then_inc(mm, 1)
                    pe.wait_ge(relu, b + 1)

            @block.vector
            def _(dve):
                v = nc.vector
                dve.wait_ge(consts_in, 16 * 7)
                with dve.Fori(0, z.NB) as b:
                    dve.wait_ge(relu, b + 1)
                    v.tensor_tensor(hp[:, :, :], h[:, :, :], av[:, :].unsqueeze(1).to_broadcast([P, TB, 3 * D]), ALU.mult)
                    dve.drain()
                    v.tensor_reduce(f3[:, :, :].rearrange("p t j -> p (t j)"),
                                    hp[:, :, :].rearrange("p t (j d) -> p (t j) d", d=D), AX, ALU.add).then_inc(feats, 1)
                    dve.wait_ge(sig, b + 1)
                    for i in range(3):
                        v.tensor_tensor(l9[:, :, i * 3:(i + 1) * 3], g3[:, :, i:i + 1].to_broadcast([P, TB, 3]),
                                        att_vec[:, i * 3:(i + 1) * 3].unsqueeze(1).to_broadcast([P, TB, 3]), ALU.mult)
                    dve.drain()
                    v.tensor_tensor(f3[:, :, :], l9[:, :, 0:3], l9[:, :, 3:6], ALU.add)
                    dve.drain()
                    v.tensor_tensor(f3[:, :, :], f3[:, :, :], l9[:, :, 6:9], ALU.add)
                    dve.drain()
                    v.tensor_reduce(m1[:, :], f3[:, :, :], AX, ALU.max)
                    dve.drain()
                    v.tensor_tensor(f3[:, :, :], f3[:, :, :], m1[:, :].unsqueeze(2).to_broadcast([P, TB, 3]),
                                    ALU.subtract).then_inc(logit, 1)
                    dve.wait_ge(expd, b + 1)
                    v.tensor_reduce(m1[:, :], g3[:, :, :], AX, ALU.add)
                    dve.drain()
                    v.reciprocal(m1[:, :], m1[:, :])
                    dve.drain()
                    v.tensor_scalar(m1[:, :], m1[:, :], 3.0, None, ALU.mult)
                    dve.drain()
                    v.tensor_tensor(g3[:, :, :], g3[:, :, :], m1[:, :].unsqueeze(2).to_broadcast([P, TB, 3]), ALU.mult)
                    dve.drain()
                    v.tensor_tensor(hp[:, :, :].rearrange("p t (j d) -> p (t j) d", d=D),
                                    h[:, :, :].rearrange("p t (j d) -> p (t j) d", d=D),
                                    g3[:, :, :].rearrange("p t j -> p (t j)").unsqueeze(2).to_broadcast([P, TB * 3, D]), ALU.mult)
                    dve.drain()
                    dve.wait_ge(x_in, b * 16 + 16)
                    v.tensor_tensor(y[:, :, :], xb[:, :, :], hp[:, :, 0:D], ALU.add)
                    dve.drain()
                    v.tensor_tensor(y[:, :, :], y[:, :, :], hp[:, :, D:2 * D], ALU.add)
                    dve.drain()
                    v.tensor_tensor(y[:, :, :], y[:, :, :], hp[:, :, 2 * D:3 * D], ALU.add)
                    norm_vector(nc, dve, k, y, s, b, eps_in, eps_out, done)


def write_out(nc, z, k, out):
    with ExitStack() as ctx:
        sb, ps, sem = make(nc, ctx)
        out_done = sem("out_done")
        full, rest = z.n // P, z.n % P
        with nc.Block() as block:

            @block.sync
            def _(sp):
                sp.dma_start(out[0:full * P, :].rearrange("(t p) d -> p t d", p=P),
                             k.x[:, 0:full * D].rearrange("p (t d) -> p t d", d=D)).then_inc(out_done, 16)
                if rest:
                    sp.dma_start(out[full * P:z.n, :], k.x[0:rest, full * D:(full + 1) * D]).then_inc(out_done, 16)
                sp.wait_ge(out_done, 16 + 16 * (rest > 0))
                sp.wait_ge(k.sync_groups, 6 * z.G)
                sp.wait_ge(k.pool_groups, 3 * z.G)


def layer1(nc, z, k, a):
    with ExitStack() as ctx:
        sb, ps, sem = make(nc, ctx)
        k.off = sb("off", [P, z.NT])
        k.end_i = sb("end_i", [P, z.NT], i32)
        k.end = sb("end", [P, z.NT])
        layer1_places(nc, z, k, a)
        layer1_scatter(nc, z, k, a)
        layer1_scan(nc, z, k, a)
        layer1_nodes(nc, z, k, a)


def layer1_places(nc, z, k, a):
    with ExitStack() as ctx:
        sb, ps, sem = make(nc, ctx)
        incl = sb("incl", [P, z.NT])
        below = ps("below", [P, z.NT])
        total = ps("total", [P, z.NT])
        sums = sem("place_sums")
        with nc.Block() as block:

            @block.tensor
            def _(pe):
                nc.tensor.matmul(below[:, :], k.after[:, :], k.cnt_src[:, :], start=True, stop=True).then_inc(sums, 1)
                nc.tensor.matmul(total[:, :], k.ones[:, :], k.cnt_src[:, :], start=True, stop=True).then_inc(sums, 1)

            @block.vector
            def _(dve):
                v = nc.vector
                dve.wait_ge(sums, 2)
                v.tensor_tensor_scan(incl[:, :], k.ones[:, 0:z.NT], total[:, :], 0.0, ALU.mult, ALU.add)
                dve.drain()
                v.tensor_tensor(incl[:, :], incl[:, :], total[:, :], ALU.subtract)
                dve.drain()
                v.tensor_tensor(k.off[:, :], below[:, :], incl[:, :], ALU.add)
                dve.drain()
                v.tensor_tensor(k.end[:, :], k.off[:, :], k.cnt_src[:, :], ALU.add)
                dve.drain()
                v.tensor_scalar(k.end[:, :], k.end[:, :], -1.0, None, ALU.add)
                dve.drain()
                v.tensor_scalar(k.end_i[:, :], k.end[:, :], 0.0, None, ALU.max)
                dve.drain()


def layer1_scatter(nc, z, k, a):
    NT, HB = z.NT, CH // 2
    QC = 4
    with ExitStack() as ctx:
        sb, ps, sem = make(nc, ctx)
        hilo = [sb(f"hilo{b}", [2, GE], bf16) for b in range(2)]
        row = [sb(f"row{b}", [P, CH, RW]) for b in range(2)]
        hot_lo = [sb(f"s_hot_lo{b}", [P, CH, P], bf16) for b in range(2)]
        hot_hi = [sb(f"s_hot_hi{b}", [P, CH, NT], bf16) for b in range(2)]
        lo_hot = [sb(f"lo_hot{b}", [P, CH * P]) for b in range(2)]
        apart = [sb(f"apart{b}", [P, CH * P]) for b in range(2)]
        minus_p = sb("minus_p", [P, 1])
        inner = [sb(f"inner{b}", [P, CH]) for b in range(2)]
        place = [sb(f"place{b}", [P, CH], i32) for b in range(2)]
        running = sb("running", [P, CH + 1, NT])
        prod = sb("prod", [P, CH, NT])
        outer = sb("outer", [P, CH])
        junk = sb("junk", [P, CH, P], bf16)
        delta = ps("delta", [P, 2, 512])
        found = ps("found", [P, 2, 512])
        key_bc = [ps(f"key_bc{b}", [P, QC * P]) for b in range(2)]
        lo_bc = [ps(f"lo_bc{b}", [P, QC * P]) for b in range(2)]
        hilo_in = [sem(f"hilo_in{b}") for b in range(2)]
        row_in = [sem(f"row_in{b}") for b in range(2)]
        rows_out = [sem(f"rows_out{b}") for b in range(2)]
        hot_ready, bc_ready, key_used, lo_used, lo_ready, delta_ready, added, found_ready, place_ready, sent, minus_set = (
            sem(n) for n in ("s_hot_ready", "bc_ready", "key_used", "lo_used", "lo_ready", "delta_ready", "counts_added",
                             "found_ready", "place_ready", "scatter_starts", "minus_set"))
        hv = a["hilo_d"].rearrange("r (g e) -> g r e", g=z.G)
        ev = a["ea"].rearrange("(g p c) f -> g p c f", p=P, c=CH)
        with nc.Block() as block:

            @block.sync
            def _(sp):
                def group(g, b):
                    wait(sp, bc_ready, (g - 1) * 4)
                    sp.sem_inc(k.sync_groups, 1)
                    sp.dma_start(hilo[b][:, :], hv[at(g)].rearrange("g r e -> (g r) e")).then_inc(hilo_in[b], 16)
                    if not (isinstance(g, int) and g < 2):
                        sp.wait_ge(rows_out[b], (g - b) * (CH * 8))
                    sp.sem_inc(k.sync_groups, 1)
                    sp.dma_start(row[b][:, :, 0:F], ev[at(g)].rearrange("g p c f -> (g p) c f")).then_inc(row_in[b], 16)
                over_groups(sp, z.G, group)
                for b in range(2):
                    sp.wait_ge(rows_out[b], (z.G + 1 - b) // 2 * CH * 16)

            @block.gpsimd
            def _(pool):
                def group(g, b):
                    pool.wait_ge(row_in[b], (g - b) * 8 + 16)
                    pool.wait_ge(place_ready, g * 2 + 2)
                    pool.sem_inc(sent, 1)
                    for c in range(CH):
                        pool.indirect_dma_start(a["sorted_d"][:, :], bass.IndirectOffsetOnAxis(ap=place[b][:, c:c + 1], axis=0),
                                                row[b][:, c, :], None).then_inc(rows_out[b], 16)
                over_groups(pool, z.G, group)
                pool.wait_ge(sent, z.G)

            @block.vector
            def _(dve):
                v = nc.vector
                v.tensor_scalar(minus_p[:, :], k.iota_p[:, :], -1.0, None, ALU.mult).then_inc(minus_set, 1)
                v.tensor_copy(running[:, CH, :], k.off[:, :])
                dve.drain()

                def places(g, b):
                    if not (isinstance(g, int) and g < 2):
                        dve.wait_ge(rows_out[b], (g - b) * (CH * 8))
                    v.tensor_scalar(row[b][:, :, F], k.src[:, at(g, CH)], 1.0, None, ALU.mult).then_inc(place_ready, 1)
                    dve.wait_ge(found_ready, g + 1)
                    v.tensor_tensor(prod[:, :, :].rearrange("p (h c) n -> p h (c n)", h=2),
                                    found[:, :, 0:HB * NT],
                                    hot_hi[b][:, :, :].rearrange("p (h c) n -> p h (c n)", h=2), ALU.mult)
                    dve.drain()
                    v.tensor_reduce(outer[:, :], prod[:, :, :], AX, ALU.add)
                    dve.drain()
                    v.tensor_tensor(place[b][:, :], outer[:, :], inner[b][:, :], ALU.add).then_inc(place_ready, 1)

                def group(g, b):
                    v.tensor_tensor(hot_lo[b][:, :, :], k.iota[:, :].unsqueeze(1).to_broadcast([P, CH, P]),
                                    k.src_lo[:, at(g, CH)].unsqueeze(2).to_broadcast([P, CH, P]),
                                    ALU.is_equal).then_inc(hot_ready, 1)
                    v.tensor_tensor(hot_hi[b][:, :, :], k.iota[:, 0:NT].unsqueeze(1).to_broadcast([P, CH, NT]),
                                    k.src_hi[:, at(g, CH)].unsqueeze(2).to_broadcast([P, CH, NT]),
                                    ALU.is_equal).then_inc(hot_ready, 1)
                    if not (isinstance(g, int) and g < 1):
                        places(g - 1, 1 - b)
                    for q in range(CH // QC):
                        dve.wait_ge(bc_ready, g * 4 + (q + 1))
                        for c in range(QC):
                            col = k.src[:, bass.ds(g * CH + (q * QC + c), 1)]
                            last = v.scalar_tensor_tensor(out=junk[:, q * QC + c, :], in0=key_bc[q % 2][:, c * P:(c + 1) * P],
                                                          scalar=col, in1=k.before[:, :], op0=ALU.is_equal, op1=ALU.mult,
                                                          accum_out=inner[b][:, q * QC + c:q * QC + c + 1])
                            last.then_inc(key_used, 1)
                    dve.wait_ge(delta_ready, g + 1)
                    v.tensor_copy(running[:, 0, :], running[:, CH, :]).then_inc(added, 1)
                    for c in range(CH):
                        o = (c % HB) * NT
                        dve.wait_ge(added, g * (CH + 1) + (c + 1))
                        v.tensor_tensor(running[:, c + 1, :], running[:, c, :], delta[:, c // HB, o:o + NT], ALU.add).then_inc(added, 1)
                over_groups(dve, z.G, group)
                places(z.G - 1, (z.G - 1) % 2)

            @block.scalar
            def _(act):
                sc = nc.scalar

                def group(g, b):
                    wait(act, found_ready, g - 1)
                    for q in range(CH // QC):
                        part = slice(q * QC * P, (q + 1) * QC * P)
                        act.wait_ge(bc_ready, g * 4 + (q + 1))
                        sc.activation(apart[b][:, part], lo_bc[q % 2][:, :], ACT.Abs, bias=minus_p[:, 0:1]).then_inc(lo_used, 1)
                        act.wait_ge(lo_used, g * 4 + (q + 1))
                        sc.activation(lo_hot[b][:, part], apart[b][:, part], ACT.Relu, bias=1.0, scale=-1.0).then_inc(lo_ready, 1)
                act.wait_ge(minus_set, 1)
                over_groups(act, z.G, group)

            @block.tensor
            def _(pe):
                def group(g, b):
                    def numbers(q):
                        wait(pe, key_used, g * CH + (q - 1) * QC)
                        wait(pe, lo_used, g * 4 + (q - 1))
                        src = hilo[b][:, :].rearrange("r (p c) -> r c p", c=CH)[:, q * QC:(q + 1) * QC, :]
                        nc.tensor.matmul(key_bc[q % 2][:, :], k.pick[:, 0, :], src, start=True, stop=True)
                        nc.tensor.matmul(lo_bc[q % 2][:, :], k.pick[:, 1, :], src, start=True, stop=True).then_inc(bc_ready, 1)
                    pe.wait_ge(hilo_in[b], (g - b) * 8 + 16)
                    numbers(0)
                    numbers(1)
                    wait(pe, added, g * (CH + 1))
                    pe.wait_ge(hot_ready, g * 2 + 2)
                    for c in range(CH):
                        o = (c % HB) * NT
                        last = nc.tensor.matmul(delta[:, c // HB, o:o + NT], hot_lo[b][:, c, :], hot_hi[b][:, c, :],
                                                start=True, stop=True)
                    last.then_inc(delta_ready, 1)
                    numbers(2)
                    numbers(3)
                    pe.wait_ge(lo_ready, g * 4 + 4)
                    for h in range(2):
                        pe.wait_ge(added, g * (CH + 1) + (h + 1) * HB)
                        for c in range(h * HB, (h + 1) * HB):
                            o = (c % HB) * NT
                            last = nc.tensor.matmul(found[:, h, o:o + NT], lo_hot[b][:, c * P:(c + 1) * P], running[:, c, :],
                                                    start=True, stop=True)
                    last.then_inc(found_ready, 1)
                over_groups(pe, z.G, group)


def layer1_scan(nc, z, k, a):
    TU = 4
    S = TU * P
    with ExitStack() as ctx:
        sb, ps, sem = make(nc, ctx)
        ld = [sb(f"ld{b}", [P, 4, TU * RW]) for b in range(2)]
        val_w = [sb(f"val_w{b}", [P, TU, 4, F]) for b in range(2)]
        key_w = [sb(f"key_w{b}", [P, TU, 4, F]) for b in range(2)]
        keys = [sb(f"keys{b}", [P, S + 1]) for b in range(2)]
        same = [sb(f"same{b}", [P, S]) for b in range(2)]
        cut = [sb(f"cut{b}", [P, S]) for b in range(2)]
        sums = [sb(f"sums{b}", [P, S]) for b in range(2)]
        maxs = [sb(f"maxs{b}", [P, S]) for b in range(2)]
        st = [sb(f"st{b}", [P, 4, TU, 2 * F]) for b in range(2)]
        val_t = [ps(f"val_t{b}", [P, S]) for b in range(2)]
        key_t = ps("key_t", [P, S])
        back = ps("back", [P, 2, S])
        ld_in = [sem(f"ld_in{b}") for b in range(2)]
        st_out = [sem(f"st_out{b}") for b in range(2)]
        laid, key_laid, turned, keys_ready, same_ready, cut_ready, scanned, back_ready, st_ready, starts = (
            sem(n) for n in ("laid_out", "key_laid_out", "turned", "keys_ready", "same_ready", "cut_ready", "scanned", "back_ready", "st_ready", "store_starts"))
        lv = a["sorted_d"].rearrange("(q j p i) w -> j p q (i w)", q=4, p=P, i=TU)
        ov = a["scan_d"].rearrange("(q j p i) w -> j p q (i w)", q=4, p=P, i=TU)
        with nc.Block() as block:

            @block.sync
            def _(sp):
                def step(j, b):
                    wait(sp, laid, j - 1)
                    wait(sp, key_laid, j - 1)
                    sp.sem_inc(k.sync_groups, 1)
                    sp.dma_start(ld[b][:, :, :], lv[at(j)].rearrange("j p q w -> (j p) q w")).then_inc(ld_in[b], 16)
                over_groups(sp, z.G, step)

            @block.gpsimd
            def _(pool):
                def store(j, b):
                    pool.wait_ge(st_ready, j * 2 + 2)
                    pool.sem_inc(starts, 1)
                    pool.dma_start(ov[at(j)].rearrange("j p q w -> (j p) q w"),
                                   st[b][:, :, :, :].rearrange("p q i w -> p q (i w)")).then_inc(st_out[b], 16)

                def step(j, b):
                    pool.wait_ge(ld_in[b], (j - b) * 8 + 16)
                    wait(pool, turned, j - 1)
                    pool.sem_inc(starts, 1)
                    rows = ld[b][:, :, :].rearrange("p q (i w) -> p i q w", w=RW)
                    pool.tensor_copy(val_w[b][:, :, :, :], rows[:, :, :, 0:F]).then_inc(laid, 1)
                    if not (isinstance(j, int) and j < 2):
                        store(j - 2, b)
                over_groups(pool, z.G, step)
                for j in range(max(z.G - 2, 0), z.G):
                    store(j, j % 2)
                for b in range(2):
                    pool.wait_ge(st_out[b], (z.G + 1 - b) // 2 * 16)
                pool.wait_ge(starts, 2 * z.G)

            @block.tensor
            def _(pe):
                def turn_back(j, b):
                    pe.wait_ge(scanned, j * 2 + 2)
                    wait(pe, st_ready, j * 2)
                    for s, scan in enumerate((sums[b], maxs[b])):
                        for i in range(TU):
                            last = nc.tensor.transpose(back[:, s, i * P:(i + 1) * P], scan[:, i:S:TU], k.ident[:, :])
                    last.then_inc(back_ready, 1)

                def step(j, b):
                    pe.wait_ge(laid, j + 1)
                    pe.wait_ge(key_laid, j + 1)
                    wait(pe, keys_ready, j)
                    wait(pe, scanned, (j - 1) * 2)
                    for i in range(TU):
                        nc.tensor.transpose(key_t[:, i:S:TU], key_w[b][:, i].rearrange("p q f -> p (q f)"), k.ident[:, :])
                        last = nc.tensor.transpose(val_t[b][:, i:S:TU], val_w[b][:, i].rearrange("p q f -> p (q f)"), k.ident[:, :])
                    last.then_inc(turned, 1)
                    if not (isinstance(j, int) and j < 1):
                        turn_back(j - 1, 1 - b)
                over_groups(pe, z.G, step)
                turn_back(z.G - 1, (z.G - 1) % 2)

            @block.scalar
            def _(act):
                sc = nc.scalar

                def copy_out(j, b):
                    act.wait_ge(back_ready, j + 1)
                    if not (isinstance(j, int) and j < 2):
                        act.wait_ge(st_out[b], (j - b) * 8)
                    for s in range(2):
                        sc.activation(st[b][:, :, :, s * F:(s + 1) * F].rearrange("p q i f -> p i q f"),
                                      back[:, s, :].rearrange("p (i q f) -> p i q f", q=4, f=F), ACT.Copy).then_inc(st_ready, 1)

                def scan_inputs(j, b):
                    act.wait_ge(turned, j + 1)
                    wait(act, same_ready, j)
                    if isinstance(j, int) and j == 0:
                        sc.activation(keys[0][:, 0:1], k.ones[:, 0:1], ACT.Copy, scale=-1.0)
                    else:
                        sc.activation(keys[b][:, 0:1], keys[1 - b][:, S:S + 1], ACT.Copy)
                    sc.activation(keys[b][:, 1:S + 1], key_t[:, :], ACT.Copy).then_inc(keys_ready, 1)
                    act.wait_ge(same_ready, j + 1)
                    wait(act, scanned, (j - 1) * 2)
                    sc.activation(cut[b][:, :], same[b][:, :], ACT.Copy, bias=-BIG, scale=BIG).then_inc(cut_ready, 1)
                    if not (isinstance(j, int) and j < 1):
                        copy_out(j - 1, 1 - b)

                def step(j, b):
                    act.wait_ge(ld_in[b], (j - b) * 8 + 16)
                    rows = ld[b][:, :, :].rearrange("p q (i w) -> p i q w", w=RW)
                    sc.activation(key_w[b][:, :, :, :], rows[:, :, :, F:RW].to_broadcast([P, TU, 4, F]),
                                  ACT.Copy).then_inc(key_laid, 1)
                    if not (isinstance(j, int) and j < 1):
                        scan_inputs(j - 1, 1 - b)
                over_groups(act, z.G, step)
                scan_inputs(z.G - 1, (z.G - 1) % 2)
                copy_out(z.G - 1, (z.G - 1) % 2)

            @block.vector
            def _(dve):
                v = nc.vector

                def step(j, b):
                    dve.wait_ge(keys_ready, j + 1)
                    v.tensor_tensor(same[b][:, :], keys[b][:, 1:S + 1], keys[b][:, 0:S], ALU.is_equal).then_inc(same_ready, 1)
                    dve.drain()
                    wait(dve, back_ready, j - 1)
                    first = isinstance(j, int) and j == 0
                    v.tensor_tensor_scan(sums[b][:, :], same[b][:, :], val_t[b][:, :],
                                         0.0 if first else sums[1 - b][:, S - 1:S], ALU.mult, ALU.add).then_inc(scanned, 1)
                    dve.wait_ge(cut_ready, j + 1)
                    v.tensor_tensor_scan(maxs[b][:, :], cut[b][:, :], val_t[b][:, :],
                                         0.0 if first else maxs[1 - b][:, S - 1:S], ALU.add, ALU.max).then_inc(scanned, 1)
                over_groups(dve, z.G, step)


def layer1_nodes(nc, z, k, a):
    Z = 3 * F + 2
    with ExitStack() as ctx:
        sb, ps, sem = make(nc, ctx)
        ends = sb("ends", [P, z.NT, 2 * F])
        edge = sb("edge", [P, 3, 2 * F])
        w1 = sb("l1_w1", [Z, HID])
        w2 = sb("l1_w2", [HID, D])
        b2 = sb("l1_b2", [P, D])
        u = sb("l1_u", [P, 1])
        zb = sb("zb", [P, TB, Z])
        zt = sb("zt", [Z, TB * P])
        ht = sb("ht", [HID, TB * P])
        in_q = sb("in_q", [P, z.NT, 3])
        pen_q = sb("pen_q", [P, z.NT, 3])
        some = sb("some", [P, z.NT])
        inv = sb("inv", [P, z.NT])
        t1 = sb("t1", [P, z.NT])
        tmp = sb("tmp", [P, TB, 2 * F])
        y = sb("y1", [P, TB, D])
        s = sb("s1", [P, 3 * TB])
        zt_ps = ps("zt_ps", [Z, 2, 512])
        ht_ps = ps("ht_ps", [HID, 2, 512])
        o_ps = ps("o_ps", [P, TB * D])
        consts_in, ends_in, zb_ready, zt_ready, zt_copied, ht_ready, ht_copied, o_ready, eps_in, eps_out, done = (
            sem(n) for n in ("l1_consts", "ends_in", "zb_ready", "zt_ready", "zt_copied", "ht_ready", "ht_copied",
                             "o_ready", "l1_var_ready", "l1_std_ready", "x2_ready"))
        halves = ((0, 4), (4, TB))
        with nc.Block() as block:

            @block.sync
            def _(sp):
                sp.dma_start(w1[0:Z - 1, :], a["L1_gnn_W1"]).then_inc(consts_in, 16)
                sp.dma_start(w1[Z - 1:Z, :], a["L1_gnn_b1"].rearrange("(a h) -> a h", a=1)).then_inc(consts_in, 16)
                sp.dma_start(w2[:, :], a["L1_gnn_W2"]).then_inc(consts_in, 16)
                sp.dma_start(b2[:, :], a["L1_gnn_b2"].rearrange("(a h) -> a h", a=1).to_broadcast([P, D])).then_inc(consts_in, 16)
                sp.dma_start(u[:, :], a["L1_gnn_u"][0:1, :].to_broadcast([P, 1])).then_inc(consts_in, 16)
                sp.dma_start(edge[:, :, :], a["scan_d"].rearrange("(q e) w -> q e w", q=4)[0:3, z.EP // 4 - 1, :]
                             .unsqueeze(0).to_broadcast([P, 3, 2 * F])).then_inc(consts_in, 16)

            @block.gpsimd
            def _(pool):
                for t in range(z.NT):
                    pool.indirect_dma_start(ends[:, t, :], None, a["scan_d"][:, :],
                                            bass.IndirectOffsetOnAxis(ap=k.end_i[:, t:t + 1], axis=0)).then_inc(ends_in, 16)

            @block.vector
            def _(dve):
                v = nc.vector
                for q in range(3):
                    edge_at = float((q + 1) * (z.EP // 4))
                    v.tensor_scalar(in_q[:, :, q], k.off[:, :], edge_at, None, ALU.is_lt)
                    v.tensor_scalar(t1[:, :], k.end[:, :], edge_at, None, ALU.is_ge)
                    dve.drain()
                    v.tensor_tensor(in_q[:, :, q], in_q[:, :, q], t1[:, :], ALU.mult)
                    dve.drain()
                v.tensor_scalar(pen_q[:, :, :], in_q[:, :, :], -1.0, BIG, ALU.add, ALU.mult)
                v.tensor_scalar(some[:, :], k.cnt_src[:, :], 0.0, None, ALU.is_gt)
                v.tensor_scalar(inv[:, :], k.cnt_src[:, :], 1.0, None, ALU.max)
                dve.drain()
                v.reciprocal(inv[:, :], inv[:, :])
                dve.wait_ge(consts_in, 16 * 6)
                v.tensor_copy(zb[:, :, 3 * F], u[:, 0:1].to_broadcast([P, TB]))
                v.memset(zb[:, :, 3 * F + 1], 1.0)
                dve.wait_ge(ends_in, 16 * z.NT)

                def features(b):
                    v.tensor_scalar(zb[:, :, 0:2 * F], ends[:, at(b, TB), :], 1.0, None, ALU.mult)
                    for q in range(3):
                        dve.drain()
                        v.tensor_tensor(tmp[:, :, 0:F], in_q[:, at(b, TB), q:q + 1].to_broadcast([P, TB, F]),
                                        edge[:, q, 0:F].unsqueeze(1).to_broadcast([P, TB, F]), ALU.mult)
                        v.tensor_tensor(tmp[:, :, F:2 * F], pen_q[:, at(b, TB), q:q + 1].to_broadcast([P, TB, F]),
                                        edge[:, q, F:2 * F].unsqueeze(1).to_broadcast([P, TB, F]), ALU.add)
                        dve.drain()
                        v.tensor_tensor(zb[:, :, 0:F], zb[:, :, 0:F], tmp[:, :, 0:F], ALU.add)
                        v.tensor_tensor(zb[:, :, F:2 * F], zb[:, :, F:2 * F], tmp[:, :, F:2 * F], ALU.max)
                    dve.drain()
                    v.tensor_tensor(zb[:, :, 0:2 * F], zb[:, :, 0:2 * F],
                                    some[:, at(b, TB)].unsqueeze(2).to_broadcast([P, TB, 2 * F]), ALU.mult)
                    dve.drain()
                    v.tensor_tensor(zb[:, :, 2 * F:3 * F], zb[:, :, 0:F],
                                    inv[:, at(b, TB)].unsqueeze(2).to_broadcast([P, TB, F]), ALU.mult).then_inc(zb_ready, 1)

                def block_(b, more):
                    if more:
                        dve.drain()
                        dve.wait_ge(zt_ready, b + 1)
                        features(b + 1)
                    dve.wait_ge(o_ready, b + 1)
                    v.tensor_tensor(y[:, :, :], o_ps[:, :].rearrange("p (t d) -> p t d", d=D),
                                    b2[:, :].unsqueeze(1).to_broadcast([P, TB, D]), ALU.add)
                    dve.drain()
                    v.tensor_tensor(y[:, :, :], y[:, :, :],
                                    k.x[:, at(b, TB * D)].rearrange("p (t d) -> p t d", d=D), ALU.add)
                    norm_vector(nc, dve, k, y, s, b, eps_in, eps_out, done)
                features(0)
                over_blocks(dve, z.NB, block_)

            @block.tensor
            def _(pe):
                pe.wait_ge(consts_in, 16 * 6)
                with pe.Fori(0, z.NB) as b:
                    pe.wait_ge(zb_ready, b + 1)
                    for t in range(TB):
                        last = nc.tensor.transpose(zt_ps[:, t // 4, (t % 4) * P:(t % 4 + 1) * P], zb[:, t, :], k.ident[:, :])
                    last.then_inc(zt_ready, 1)
                    pe.wait_ge(zt_copied, b * 2 + 2)
                    for h, (t0, t1_) in enumerate(halves):
                        last = nc.tensor.matmul(ht_ps[:, h, 0:(t1_ - t0) * P], w1[:, :], zt[:, t0 * P:t1_ * P], start=True, stop=True)
                    last.then_inc(ht_ready, 1)
                    pe.wait_ge(ht_copied, b * 2 + 2)
                    for t in range(TB):
                        last = nc.tensor.matmul(o_ps[:, t * D:(t + 1) * D], ht[:, t * P:(t + 1) * P], w2[:, :], start=True, stop=True)
                    last.then_inc(o_ready, 1)

            @block.scalar
            def _(act):
                sc = nc.scalar
                with act.Fori(0, z.NB) as b:
                    act.wait_ge(zt_ready, b + 1)
                    for h, (t0, t1_) in enumerate(halves):
                        sc.activation(zt[:, t0 * P:t1_ * P], zt_ps[:, h, 0:(t1_ - t0) * P], ACT.Copy).then_inc(zt_copied, 1)
                    act.wait_ge(ht_ready, b + 1)
                    for h, (t0, t1_) in enumerate(halves):
                        sc.activation(ht[:, t0 * P:t1_ * P], ht_ps[:, h, 0:(t1_ - t0) * P], ACT.Relu).then_inc(ht_copied, 1)
                    norm_scalar(nc, act, s, b, eps_in, eps_out)


def block_of(k, b):
    return k.x[:, at(b, TB * D)].rearrange("p (t d) -> p t d", d=D)


def layer2(nc, z, k, a):
    with ExitStack() as ctx:
        sb, ps, sem = make(nc, ctx)
        k.acc1 = sb("acc1", [P, z.NC])
        k.dst_gain = sb("dst_gain", [P, z.NT, 4])
        k.inv_deg = sb("inv_deg", [P, z.NT])
        layer2_tables(nc, z, k, a)
        layer2_edges(nc, z, k, a)
        layer2_nodes(nc, z, k, a)


def layer2_tables(nc, z, k, a):
    with ExitStack() as ctx:
        sb, ps, sem = make(nc, ctx)
        mu = sb("mu", [P, 4, 2])
        sigma = sb("sigma", [P, 4, 2])
        coef = sb("coef", [P, 4, 2])
        root = sb("root_deg", [P, z.NT])
        diff = sb("diff", [P, 2, z.NT, 4])
        gain = sb("gain", [P, 2, z.NT, 4])
        scaled = [sb(f"scaled{b}", [P, TB, 4, D]) for b in range(2)]
        consts_in, deg_ready, root_ready, diff_ready, gain_ready, scaled_ready, starts = (
            sem(n) for n in ("l2_consts", "deg_ready", "root_ready", "diff_ready", "gain_ready", "scaled_ready", "l2_starts"))
        table_out = [sem(f"table_out{b}") for b in range(2)]
        yv = a["gains_d"].rearrange("(b t p) w -> b p t w", p=P, t=TB)
        with nc.Block() as block:

            @block.sync
            def _(sp):
                sp.dma_start(mu[:, :, :], a["L2_gnn_mu"].unsqueeze(0).to_broadcast([P, 4, 2])).then_inc(consts_in, 16)
                sp.dma_start(sigma[:, :, :], a["L2_gnn_sigma"].unsqueeze(0).to_broadcast([P, 4, 2])).then_inc(consts_in, 16)
                for b in range(z.NB):
                    sp.wait_ge(scaled_ready, 4 * (b + 1))
                    sp.dma_start(yv[b], scaled[b % 2][:, :, :, :].rearrange("p t k d -> p t (k d)")).then_inc(table_out[b % 2], 16)
                for b in range(2):
                    wait(sp, table_out[b], (z.NB + 1 - b) // 2 * 16)

            @block.scalar
            def _(act):
                act.wait_ge(deg_ready, 1)
                nc.scalar.activation(root[:, :], root[:, :], ACT.Sqrt).then_inc(root_ready, 1)
                act.wait_ge(diff_ready, 2)
                nc.scalar.activation(gain[:, :, :, :], diff[:, :, :, :], ACT.Exp).then_inc(gain_ready, 1)

            @block.vector
            def _(dve):
                v = nc.vector
                v.memset(k.acc0[:, :], 0.0)
                v.memset(k.acc1[:, :], 0.0)
                v.tensor_scalar(root[:, :], k.cnt_dst[:, :], 1.0, None, ALU.max)
                dve.drain()
                v.reciprocal(k.inv_deg[:, :], root[:, :]).then_inc(deg_ready, 1)
                dve.wait_ge(consts_in, 32)
                v.tensor_tensor(coef[:, :, :], sigma[:, :, :], sigma[:, :, :], ALU.mult)
                dve.drain()
                v.tensor_scalar(coef[:, :, :], coef[:, :, :], 1e-15, None, ALU.add)
                dve.drain()
                v.reciprocal(coef[:, :, :], coef[:, :, :])
                dve.drain()
                v.tensor_scalar(coef[:, :, :], coef[:, :, :], -0.5, None, ALU.mult)
                dve.wait_ge(root_ready, 1)
                v.reciprocal(root[:, :], root[:, :])
                dve.drain()
                for s in range(2):
                    v.tensor_tensor(diff[:, s], root[:, :].unsqueeze(2).to_broadcast([P, z.NT, 4]),
                                    mu[:, :, s].unsqueeze(1).to_broadcast([P, z.NT, 4]), ALU.subtract)
                    dve.drain()
                    v.tensor_tensor(diff[:, s], diff[:, s], diff[:, s], ALU.mult)
                    dve.drain()
                    v.tensor_tensor(diff[:, s], diff[:, s],
                                    coef[:, :, s].unsqueeze(1).to_broadcast([P, z.NT, 4]), ALU.mult).then_inc(diff_ready, 1)
                dve.wait_ge(gain_ready, 1)
                v.tensor_copy(k.dst_gain[:, :, :], gain[:, 1])
                for b in range(z.NB):
                    wait(dve, table_out[b % 2], b // 2 * 16)
                    for kk in range(4):
                        v.tensor_tensor(scaled[b % 2][:, :, kk, :], block_of(k, b),
                                        gain[:, 0, b * TB:(b + 1) * TB, kk:kk + 1].to_broadcast([P, TB, D]),
                                        ALU.mult).then_inc(scaled_ready, 1)


def layer2_edges(nc, z, k, a):
    with ExitStack() as ctx:
        sb, ps, sem = make(nc, ctx)
        idx = [sb(f"g_idx{b}", [P, CH], i32) for b in range(2)]
        rows = [sb(f"g_rows{b}", [P, CH, 4 * D]) for b in range(2)]
        onehot = sb("g_onehot", [P, CH, W])
        cur = sb("g_cur", [P, CH])
        win = ps("g_win", [P, 2, 512])
        idx_in = [sem(f"g_idx_in{b}") for b in range(2)]
        rows_in = [sem(f"g_rows_in{b}") for b in range(2)]
        onehot_ready, win_ready, group_done = (
            sem(n) for n in ("g_onehot_ready", "g_win_ready", "g_group_done"))
        iv = a["src"].rearrange("(g p c) -> g p c", p=P, c=CH)
        with nc.Block() as block:

            @block.sync
            def _(sp):
                def group(g, b):
                    if not (isinstance(g, int) and g < 2):
                        sp.wait_ge(rows_in[b], (g - b) * (CH * 8))
                    sp.sem_inc(k.sync_groups, 1)
                    sp.dma_start(idx[b][:, :], iv[at(g)].rearrange("g p c -> (g p) c")).then_inc(idx_in[b], 16)
                over_groups(sp, z.G, group)

            @block.gpsimd
            def _(pool):
                def group(g, b):
                    pool.wait_ge(idx_in[b], (g - b) * 8 + 16)
                    wait(pool, group_done, g - 1)
                    pool.sem_inc(k.pool_groups, 1)
                    for c in range(CH):
                        pool.indirect_dma_start(rows[b][:, c, :], None, a["gains_d"][:, :],
                                                bass.IndirectOffsetOnAxis(ap=idx[b][:, c:c + 1], axis=0)
                                                ).then_inc(rows_in[b], 16)
                over_groups(pool, z.G, group)

            @block.vector
            def _(dve):
                def group(g, b):
                    windows_vector(nc, dve, k, g, onehot, cur, [(k.acc0, win[:, 0, 0:W]), (k.acc1, win[:, 1, 0:W])],
                                   onehot_ready, win_ready, group_done)
                over_groups(dve, z.G, group)
                dve.wait_ge(group_done, z.G)

            @block.tensor
            def _(pe):
                def group(g, b):
                    def window():
                        for h in range(2):
                            for c in range(CH):
                                last = nc.tensor.matmul(win[:, h, 0:W], rows[b][:, c, h * P:(h + 1) * P], onehot[:, c, :],
                                                        start=(c == 0), stop=(c == CH - 1))
                        return last
                    windows_tensor(pe, k, g, window, onehot_ready, win_ready, rows_in[b], (g - b) * (CH * 8) + CH * 16)
                over_groups(pe, z.G, group)


def layer2_nodes(nc, z, k, a):
    with ExitStack() as ctx:
        sb, ps, sem = make(nc, ctx)
        g_w = sb("g_w", [P, 2, D])
        root_w = sb("root_w", [D, D])
        bias = sb("l2_bias", [P, D])
        agg = sb("l2_agg", [P, 2, TB * P])
        xs = sb("l2_xs", [P, TB * D])
        xt = sb("l2_xt", [D, TB * P])
        y = sb("y2", [P, TB, D])
        t = sb("l2_t", [P, TB, D])
        s = sb("s2", [P, 3 * TB])
        xt_ps = ps("l2_xt_ps", [D, 2, 512])
        pb = ps("l2_pb", [P, 5, 512])
        consts_in, staged, turned, xt_ready, mm, products_read, eps_in, eps_out, done = (
            sem(n) for n in ("l2n_consts", "l2_staged", "l2_turned", "l2_xt_ready", "l2_products", "l2_products_read", "l2_var_ready",
                             "l2_std_ready", "x3_ready"))
        halves = ((0, 4), (4, TB))
        with nc.Block() as block:

            @block.sync
            def _(sp):
                gv = a["L2_gnn_g"].rearrange("i (h two d) -> two i h d", h=2, two=2)
                for two in range(2):
                    sp.dma_start(g_w[two * D:(two + 1) * D, :, :], gv[two]).then_inc(consts_in, 16)
                sp.dma_start(root_w[:, :], a["L2_gnn_root"]).then_inc(consts_in, 16)
                sp.dma_start(bias[:, :], a["L2_gnn_bias"].rearrange("(a h) -> a h", a=1).to_broadcast([P, D])).then_inc(consts_in, 16)

            @block.scalar
            def _(act):
                sc = nc.scalar

                def stage(b):
                    sc.activation(xs[:, :], k.x[:, at(b, TB * D)], ACT.Copy).then_inc(staged, 1)
                    sc.activation(agg[:, 0, :], k.acc0[:, at(b, TB * P)], ACT.Copy).then_inc(staged, 1)
                    sc.activation(agg[:, 1, :], k.acc1[:, at(b, TB * P)], ACT.Copy).then_inc(staged, 1)

                def block_(b, more):
                    act.wait_ge(turned, b + 1)
                    for h, (t0, t1_) in enumerate(halves):
                        sc.activation(xt[:, t0 * P:t1_ * P], xt_ps[:, h, 0:(t1_ - t0) * P], ACT.Copy).then_inc(xt_ready, 1)
                    if more:
                        stage(b + 1)
                    norm_scalar(nc, act, s, b, eps_in, eps_out)
                stage(0)
                over_blocks(act, z.NB, block_)

            @block.tensor
            def _(pe):
                pe.wait_ge(consts_in, 16 * 4)
                pe.sem_inc(products_read, 1)
                with pe.Fori(0, z.NB) as b:
                    pe.wait_ge(staged, b * 3 + 3)
                    pe.wait_ge(products_read, b + 1)
                    for i in range(TB):
                        col = slice(i * P, (i + 1) * P)
                        o = slice(i * D, (i + 1) * D)
                        for kk in range(4):
                            half = slice((kk % 2) * D, (kk % 2 + 1) * D)
                            nc.tensor.matmul(pb[:, kk, o], agg[half, kk // 2, col], g_w[half, kk // 2, :], start=True, stop=True)
                    for i in range(TB):
                        last = nc.tensor.transpose(xt_ps[:, i // 4, (i % 4) * P:(i % 4 + 1) * P], xs[:, i * D:(i + 1) * D],
                                                   k.ident[:, :])
                    last.then_inc(turned, 1)
                    pe.wait_ge(xt_ready, b * 2 + 2)
                    for i in range(TB):
                        last = nc.tensor.matmul(pb[:, 4, i * D:(i + 1) * D], xt[:, i * P:(i + 1) * P], root_w[:, :],
                                                start=True, stop=True)
                    last.then_inc(mm, 1)

            @block.vector
            def _(dve):
                v = nc.vector
                dve.wait_ge(consts_in, 16 * 4)
                with dve.Fori(0, z.NB) as b:
                    dve.drain()
                    dve.wait_ge(mm, b + 1)
                    part = lambda kk: pb[:, kk, 0:TB * D].rearrange("p (t d) -> p t d", d=D)
                    for kk in range(4):
                        v.tensor_tensor(y[:, :, :] if kk == 0 else t[:, :, :], part(kk),
                                        k.dst_gain[:, at(b, TB), kk:kk + 1].to_broadcast([P, TB, D]), ALU.mult)
                        dve.drain()
                        if kk:
                            v.tensor_tensor(y[:, :, :], y[:, :, :], t[:, :, :], ALU.add)
                            dve.drain()
                    v.tensor_tensor(y[:, :, :], y[:, :, :], k.inv_deg[:, at(b, TB)].unsqueeze(2).to_broadcast([P, TB, D]), ALU.mult)
                    dve.drain()
                    v.tensor_tensor(y[:, :, :], part(4), y[:, :, :], ALU.add).then_inc(products_read, 1)
                    dve.drain()
                    v.tensor_tensor(y[:, :, :], y[:, :, :], bias[:, :].unsqueeze(1).to_broadcast([P, TB, D]), ALU.add)
                    dve.drain()
                    v.scalar_tensor_tensor(out=y[:, :, :], in0=y[:, :, :], scalar=0.0, in1=block_of(k, b), op0=ALU.max, op1=ALU.add)
                    dve.drain()
                    v.tensor_tensor(y[:, :, :], y[:, :, :], block_of(k, b), ALU.add)
                    norm_vector(nc, dve, k, y, s, b, eps_in, eps_out, done)


def layer3(nc, z, k, a):
    with ExitStack() as ctx:
        layer3_tables(nc, z, k, a)
        layer3_edges(nc, z, k, a)
        layer3_nodes(nc, z, k, a)


def layer3_tables(nc, z, k, a):
    with ExitStack() as ctx:
        sb, ps, sem = make(nc, ctx)
        w = sb("l3_w_nodes", [D + 1, 2 * D])
        xs = sb("l3_xs", [P, TB * D])
        xt = sb("l3_xt", [D + 1, TB * P])
        pq = [sb(f"pq{b}", [P, TB, 2 * D]) for b in range(2)]
        zero = sb("l3_zero", [P, 3 * D], bf16)
        parts = [sb(f"parts{b}", [P, TB, 3, D], bf16) for b in range(2)]
        left = sb("left", [P, TB, D])
        parts_ready = sem("parts_ready")
        deg_t = sb("deg_t", [z.NT, P])
        xt_ps = ps("l3_xt_ps", [D, 2, 512])
        pq_ps = ps("pq_ps", [P, 2, 512])
        deg_ps = ps("deg_ps", [z.NT, P])
        consts_in, staged, turned, xt_ready, products, pq_ready, one_set, zero_out, deg_turned, deg_ready, deg_out, deg_in = (
            sem(n) for n in ("l3_consts", "l3_staged", "l3_turned", "l3_xt_ready", "l3_products", "pq_ready", "one_set",
                             "zero_out", "deg_turned", "deg_copied", "deg_out", "deg_in"))
        pq_out = [sem(f"pq_out{b}") for b in range(2)]
        pv = a["from_src_d"].rearrange("(b t p) d -> b p t d", p=P, t=TB)
        qv = a["from_dst_d"][0:z.NP, :].rearrange("(b t p) d -> b p t d", p=P, t=TB)
        halves = ((0, 4), (4, TB))
        with nc.Block() as block:

            @block.sync
            def _(sp):
                sp.dma_start(w[0:D, 0:D], a["L3_gnn_W1"][0:D, :]).then_inc(consts_in, 16)
                sp.dma_start(w[0:D, D:2 * D], a["L3_gnn_W1"][D:2 * D, :]).then_inc(consts_in, 16)
                sp.dma_start(w[D:D + 1, 0:D], a["L3_gnn_b1"].rearrange("(a h) -> a h", a=1)).then_inc(consts_in, 16)
                sp.wait_ge(one_set, 2)
                sp.dma_start(a["from_dst_d"][z.NP:z.NC, :], zero[:, :]).then_inc(zero_out, 16)
                sp.wait_ge(deg_ready, 1)
                sp.dma_start(a["deg_d"].rearrange("(t p) -> t p", p=P), deg_t[:, :]).then_inc(deg_out, 16)
                sp.wait_ge(deg_out, 16)
                sp.wait_ge(one_set, 4)
                sp.dma_start(k.acc0[D:D + 1, 0:z.NP], a["deg_d"].rearrange("(a n) -> a n", a=1)).then_inc(deg_in, 16)
                for b in range(z.NB):
                    sp.wait_ge(pq_ready, 2 * (b + 1))
                    sp.dma_start(pv[b], pq[b % 2][:, :, 0:D]).then_inc(pq_out[b % 2], 16)
                    sp.wait_ge(parts_ready, b + 1)
                    sp.dma_start(qv[b], parts[b % 2][:, :, :, :].rearrange("p t s d -> p t (s d)")).then_inc(pq_out[b % 2], 16)
                for b in range(2):
                    wait(sp, pq_out[b], (z.NB + 1 - b) // 2 * 32)
                sp.wait_ge(zero_out, 16)
                sp.wait_ge(deg_in, 16)

            @block.vector
            def _(dve):
                v = nc.vector
                v.memset(zero[:, :], 0.0).then_inc(one_set, 1)
                v.memset(xt[D:D + 1, :], 1.0).then_inc(one_set, 1)
                v.memset(w[D:D + 1, D:2 * D], 0.0).then_inc(one_set, 1)
                v.memset(k.acc0[:, :], 0.0).then_inc(one_set, 1)
                dve.wait_ge(deg_turned, 1)
                v.tensor_copy(deg_t[:, :], deg_ps[:, :]).then_inc(deg_ready, 1)
                for b in range(z.NB):
                    part, q = parts[b % 2], pq[b % 2][:, :, D:2 * D]
                    dve.wait_ge(pq_ready, 2 * (b + 1))
                    v.tensor_copy(part[:, :, 0, :], q)
                    dve.drain()
                    v.tensor_tensor(left[:, :, :], q, part[:, :, 0, :], ALU.subtract)
                    dve.drain()
                    v.tensor_copy(part[:, :, 1, :], left[:, :, :])
                    dve.drain()
                    v.tensor_tensor(left[:, :, :], left[:, :, :], part[:, :, 1, :], ALU.subtract)
                    dve.drain()
                    v.tensor_copy(part[:, :, 2, :], left[:, :, :]).then_inc(parts_ready, 1)

            @block.scalar
            def _(act):
                sc = nc.scalar
                for b in range(z.NB):
                    wait(act, turned, b)
                    sc.activation(xs[:, :], k.x[:, b * TB * D:(b + 1) * TB * D], ACT.Copy).then_inc(staged, 1)
                    act.wait_ge(turned, b + 1)
                    wait(act, products, b)
                    for h, (t0, t1_) in enumerate(halves):
                        sc.activation(xt[0:D, t0 * P:t1_ * P], xt_ps[:, h, 0:(t1_ - t0) * P], ACT.Copy).then_inc(xt_ready, 1)
                    act.wait_ge(products, b + 1)
                    wait(act, pq_out[b % 2], b // 2 * 32)
                    for h, (t0, t1_) in enumerate(halves):
                        sc.activation(pq[b % 2][:, t0:t1_, :],
                                      pq_ps[:, h, 0:(t1_ - t0) * P].rearrange("p (t d) -> p t d", d=P), ACT.Copy).then_inc(pq_ready, 1)

            @block.tensor
            def _(pe):
                nc.tensor.transpose(deg_ps[:, :], k.cnt_dst[:, :], k.ident[:, :]).then_inc(deg_turned, 1)
                pe.wait_ge(consts_in, 16 * 3)
                pe.wait_ge(one_set, 3)
                for b in range(z.NB):
                    pe.wait_ge(staged, b + 1)
                    wait(pe, xt_ready, 2 * b)
                    for i in range(TB):
                        last = nc.tensor.transpose(xt_ps[:, i // 4, (i % 4) * P:(i % 4 + 1) * P], xs[:, i * D:(i + 1) * D],
                                                   k.ident[:, :])
                    last.then_inc(turned, 1)
                    pe.wait_ge(xt_ready, 2 * b + 2)
                    wait(pe, pq_ready, 2 * b)
                    for i in range(TB):
                        last = nc.tensor.matmul(pq_ps[:, i // 4, (i % 4) * P:(i % 4 + 1) * P], xt[:, i * P:(i + 1) * P], w[:, :],
                                                start=True, stop=True)
                    last.then_inc(products, 1)


def layer3_edges(nc, z, k, a):
    HB = CH // 2
    with ExitStack() as ctx:
        sb, ps, sem = make(nc, ctx)
        idx = [sb(f"m_idx{b}", [P, CH], i32) for b in range(2)]
        rows = [sb(f"m_rows{b}", [P, CH * D]) for b in range(2)]
        edge_t = [sb(f"edge_t{b}", [F, GE]) for b in range(2)]
        w_edge = sb("w_edge", [F, D])
        hot = sb("m_hot", [P, CH, W], bf16)
        hot_t = sb("m_hot_t", [W, CH * P], bf16)
        from_dst = sb("from_dst", [W, 3 * D], bf16)
        before_relu = [sb(f"before_relu{b}", [P, CH * D]) for b in range(2)]
        hid = [sb(f"m_hid{b}", [P, CH * D]) for b in range(2)]
        onehot = sb("m_onehot", [P, CH, W])
        cur_a = sb("cur_a", [P, CH])
        cur = sb("m_cur", [P, CH])
        zero = sb("m_zero", [P, 512], bf16)
        ident_b = sb("ident_b", [P, P], bf16)
        turn_ps = ps("turn_ps", [W, CH * P], bf16)
        pre = [ps(f"pre{b}", [P, 2, 512]) for b in range(2)]
        win = ps("m_win", [D, W])
        idx_in = [sem(f"m_idx_in{b}") for b in range(2)]
        rows_in = [sem(f"m_rows_in{b}") for b in range(2)]
        edge_in = [sem(f"edge_in{b}") for b in range(2)]
        (consts_in, hot_ready, hot_turned, hot_t_ready, dst_in, expanded, pre_ready, hid_ready,
         onehot_ready, win_ready, group_done) = (
            sem(n) for n in ("m_consts", "m_hot_ready", "hot_turned", "hot_t_ready", "dst_in",
                             "expanded", "pre_ready", "hid_ready", "m_onehot_ready", "m_win_ready", "m_group_done"))
        const_set = sem("m_const_set")
        added = sem("src_added")
        iv = a["src"].rearrange("(g p c) -> g p c", p=P, c=CH)
        with nc.Block() as block:

            @block.sync
            def _(sp):
                sp.dma_start(w_edge[:, :], a["L3_gnn_W1"][2 * D:2 * D + F, :]).then_inc(consts_in, 16)

                def group(g, b):
                    if not (isinstance(g, int) and g < 2):
                        sp.wait_ge(rows_in[b], (g - b) * (CH * 8))
                    wait(sp, pre_ready, g - 1)
                    sp.sem_inc(k.sync_groups, 1)
                    sp.dma_start(idx[b][:, :], iv[at(g)].rearrange("g p c -> (g p) c")).then_inc(idx_in[b], 16)
                    sp.dma_start(edge_t[b][:, :], a["eaT"][at(g)].rearrange("g f e -> (g f) e")).then_inc(edge_in[b], 16)
                over_groups(sp, z.G, group)

            @block.gpsimd
            def _(pool):
                def group(g, b):
                    pool.wait_ge(idx_in[b], (g - b) * 8 + 16)
                    wait(pool, added, g - 1)
                    pool.sem_inc(k.pool_groups, 1)
                    for c in range(CH):
                        pool.indirect_dma_start(rows[b][:, c * D:(c + 1) * D], None, a["from_src_d"][:, :],
                                                bass.IndirectOffsetOnAxis(ap=idx[b][:, c:c + 1], axis=0)
                                                ).then_inc(rows_in[b], 16)
                over_groups(pool, z.G, group)

            @block.vector
            def _(dve):
                v = nc.vector
                v.memset(zero[:, :], 0.0).then_inc(const_set, 1)
                v.tensor_copy(ident_b[:, :], k.ident[:, :]).then_inc(const_set, 1)

                def reduce(g):
                    windows_vector(nc, dve, k, g, onehot, cur, [(k.acc0[0:D, :], win[:, :])], onehot_ready, win_ready, group_done)

                def group(g, b):
                    base, count, before = table_row(dve, k, g)
                    v.tensor_copy(cur_a[:, :], k.rel[:, at(g, CH)])
                    with dve.Fori(0, count) as w:
                        dve.drain()
                        dve.wait_ge(hot_turned, before * 2 + w * 2 + 2)
                        for c in (0, HB):
                            v.tensor_tensor(hot[:, c:c + HB, :], k.iota[:, :].unsqueeze(1).to_broadcast([P, HB, W]),
                                            cur_a[:, c:c + HB].unsqueeze(2).to_broadcast([P, HB, W]),
                                            ALU.is_equal).then_inc(hot_ready, 1)
                        dve.drain()
                        v.tensor_scalar(cur_a[:, :], cur_a[:, :], -float(W), None, ALU.add)
                    dve.drain()
                    if not (isinstance(g, int) and g < 1):
                        reduce(g - 1)
                    dve.wait_ge(rows_in[b], (g - b) * (CH * 8) + CH * 16)
                    dve.wait_ge(pre_ready, g + 1)
                    wait(dve, hid_ready, g - 1)
                    v.tensor_tensor(before_relu[b][:, :], pre[b][:, :, :].rearrange("p h n -> p (h n)"), rows[b][:, :],
                                    ALU.add).then_inc(added, 1)
                over_groups(dve, z.G, group)
                reduce(z.G - 1)
                dve.wait_ge(group_done, z.G)

            @block.scalar
            def _(act):
                sc = nc.scalar

                def group(g, b):
                    base, count, before = table_row(act, k, g)
                    with act.Fori(0, count) as w:
                        first = (base + w * W).with_bounds(min_val=0, max_val=k.table_limits[0])
                        act.wait_ge(expanded, before + w + 1)
                        act.dma_start(from_dst[:, :], a["from_dst_d"][bass.ds(first, W), :]).then_inc(dst_in, 16)
                        for h in range(2):
                            act.wait_ge(hot_turned, before * 2 + w * 2 + 3 + h)
                            sc.activation(hot_t[:, h * HB * P:(h + 1) * HB * P], turn_ps[:, h * HB * P:(h + 1) * HB * P],
                                          ACT.Copy).then_inc(hot_t_ready, 1)
                    act.wait_ge(added, g + 1)
                    wait(act, group_done, g - 1)
                    sc.activation(hid[b][:, :], before_relu[b][:, :], ACT.Relu).then_inc(hid_ready, 1)
                over_groups(act, z.G, group)

            @block.tensor
            def _(pe):
                pe.sem_inc(hot_turned, 2)
                pe.sem_inc(expanded, 1)
                pe.wait_ge(const_set, 2)
                pe.wait_ge(consts_in, 16)

                def reduce(g, b):
                    def window():
                        for c in range(CH):
                            last = nc.tensor.matmul(win[:, :], hid[b][:, c * D:(c + 1) * D], onehot[:, c, :],
                                                    start=(c == 0), stop=(c == CH - 1))
                        return last
                    windows_tensor(pe, k, g, window, onehot_ready, win_ready, hid_ready, g + 1)

                def group(g, b):
                    wait(pe, added, g - 1)
                    pe.wait_ge(edge_in[b], (g - b) * 8 + 16)
                    for h in range(2):
                        nc.tensor.matmul(pre[b][:, h, :], zero[:, 0:P], zero[:, :], start=True, stop=False)
                    for c in range(CH):
                        o = (c % HB) * D
                        nc.tensor.matmul(pre[b][:, c // HB, o:o + D], edge_t[b][:, c * P:(c + 1) * P], w_edge[:, :],
                                         start=False, stop=False)
                    base, count, before = table_row(pe, k, g)
                    with pe.Fori(0, count) as w:
                        for h in range(2):
                            pe.wait_ge(hot_ready, before * 2 + w * 2 + 1 + h)
                            for c in range(h * HB, (h + 1) * HB):
                                last = nc.tensor.transpose(turn_ps[:, c * P:(c + 1) * P], hot[:, c, :], ident_b[:, :])
                            last.then_inc(hot_turned, 1)
                        pe.wait_ge(dst_in, (before + w + 1) * 16)
                        for h in range(2):
                            pe.wait_ge(hot_t_ready, before * 2 + w * 2 + 1 + h)
                            for c in range(h * HB, (h + 1) * HB):
                                o = (c % HB) * D
                                for s in range(3):
                                    last = nc.tensor.matmul(pre[b][:, h, o:o + D], hot_t[:, c * P:(c + 1) * P],
                                                            from_dst[:, s * D:(s + 1) * D], start=False, stop=False)
                        last.then_inc(expanded, 1)
                    for h in range(2):
                        last = nc.tensor.matmul(pre[b][:, h, :], zero[:, 0:P], zero[:, :], start=False, stop=True)
                    last.then_inc(pre_ready, 1)
                    if not (isinstance(g, int) and g < 1):
                        reduce(g - 1, 1 - b)
                over_groups(pe, z.G, group)
                reduce(z.G - 1, (z.G - 1) % 2)


def layer3_nodes(nc, z, k, a):
    GT = 4 * D
    with ExitStack() as ctx:
        sb, ps, sem = make(nc, ctx)
        w2 = sb("l3_w2", [D + 1, D])
        w_ih = sb("l3_w_ih", [D + 1, 3 * D])
        w_hh = sb("l3_w_hh", [D + 1, 3 * D])
        xs = sb("n_xs", [P, TB * D])
        xt = sb("n_xt", [D + 1, TB * P])
        hs = sb("n_hs", [D + 1, TB * P])
        agg = sb("n_agg", [D + 1, TB * P])
        rz = sb("n_rz", [P, TB, 2 * D])
        nn = sb("n_n", [P, TB, D])
        y = sb("y3", [P, TB, D])
        s = sb("s3", [P, 3 * TB])
        xt_ps = ps("n_xt_ps", [D, 2, 512])
        agg_ps = ps("n_agg_ps", [D, 2, 512])
        gates = ps("gates", [P, 4, 512])
        (consts_in, ones_set, staged, turned, copied, summed, gates_ready, rz_ready, n_ready, n_done, eps_in, eps_out, done) = (
            sem(n) for n in ("n_consts", "n_ones", "n_staged", "n_turned", "n_copied", "n_summed", "gates_ready", "rz_ready",
                             "n_ready", "n_done", "n_var_ready", "n_std_ready", "x4_ready"))
        halves = ((0, 4), (4, TB))
        with nc.Block() as block:

            @block.sync
            def _(sp):
                sp.dma_start(w2[0:D, :], a["L3_gnn_W2"]).then_inc(consts_in, 16)
                sp.dma_start(w_ih[0:D, :], a["L3_gnn_w_ih"]).then_inc(consts_in, 16)
                sp.dma_start(w_hh[0:D, :], a["L3_gnn_w_hh"]).then_inc(consts_in, 16)
                sp.dma_start(w2[D:D + 1, :], a["L3_gnn_b2"].rearrange("(a h) -> a h", a=1)).then_inc(consts_in, 16)
                sp.dma_start(w_ih[D:D + 1, :], a["L3_gnn_b_ih"].rearrange("(a h) -> a h", a=1)).then_inc(consts_in, 16)
                sp.dma_start(w_hh[D:D + 1, :], a["L3_gnn_b_hh"].rearrange("(a h) -> a h", a=1)).then_inc(consts_in, 16)

            def gate(i, lo, hi):
                o = (i % 2) * GT
                return gates[:, i // 2, o + lo:o + hi]

            def pairs(lo, hi):
                six = gates[:, 0:3, :].rearrange("p a (b n) -> p a b n", b=2)[:, :, :, lo:hi]
                return ((six, slice(0, 6)), (gates[:, 3, lo:hi], slice(6, 7)))

            @block.scalar
            def _(act):
                sc = nc.scalar

                def stage(b):
                    sc.activation(xs[:, :], k.x[:, at(b, TB * D)], ACT.Copy).then_inc(staged, 1)
                    sc.activation(hs[:, :], k.acc0[0:D + 1, at(b, TB * P)], ACT.Copy).then_inc(staged, 1)

                def copies(b):
                    act.wait_ge(turned, b + 1)
                    for h, (t0, t1_) in enumerate(halves):
                        sc.activation(xt[0:D, t0 * P:t1_ * P], xt_ps[:, h, 0:(t1_ - t0) * P], ACT.Copy).then_inc(copied, 1)
                        sc.activation(agg[0:D, t0 * P:t1_ * P], agg_ps[:, h, 0:(t1_ - t0) * P], ACT.Copy).then_inc(copied, 1)

                def block_(b, more):
                    if more:
                        stage(b + 1)
                    act.wait_ge(gates_ready, b + 1)
                    for src, tiles in pairs(0, 2 * D):
                        if tiles.start:
                            dst = rz[:, 6, :]
                        else:
                            dst = rz[:, 0:6, :].rearrange("p (a b) n -> p a b n", b=2)
                        sc.activation(dst, src, ACT.Sigmoid).then_inc(rz_ready, 1)
                    act.wait_ge(n_ready, b + 2)
                    sc.activation(nn[:, :, :], nn[:, :, :], ACT.Tanh).then_inc(n_done, 1)
                    if more:
                        copies(b + 1)
                    norm_scalar(nc, act, s, b, eps_in, eps_out)
                stage(0)
                copies(0)
                over_blocks(act, z.NB, block_)

            @block.tensor
            def _(pe):
                pe.wait_ge(consts_in, 16 * 6)
                pe.wait_ge(ones_set, 2)
                pe.sem_inc(n_ready, 1)
                with pe.Fori(0, z.NB) as b:
                    pe.wait_ge(staged, b * 2 + 2)
                    pe.sem_inc(summed, 1)
                    for h, (t0, t1_) in enumerate(halves):
                        nc.tensor.matmul(agg_ps[:, h, 0:(t1_ - t0) * P], w2[:, :], hs[:, t0 * P:t1_ * P], start=True, stop=True)
                    for i in range(TB):
                        last = nc.tensor.transpose(xt_ps[:, i // 4, (i % 4) * P:(i % 4 + 1) * P], xs[:, i * D:(i + 1) * D],
                                                   k.ident[:, :])
                    last.then_inc(turned, 1)
                    pe.wait_ge(copied, b * 4 + 4)
                    pe.wait_ge(n_ready, b + 1)
                    for i in range(TB):
                        col = slice(i * P, (i + 1) * P)
                        nc.tensor.matmul(gate(i, 0, 2 * D), agg[:, col], w_ih[:, 0:2 * D], start=True, stop=False)
                        nc.tensor.matmul(gate(i, 0, 2 * D), xt[:, col], w_hh[:, 0:2 * D], start=False, stop=True)
                        nc.tensor.matmul(gate(i, 2 * D, 3 * D), agg[:, col], w_ih[:, 2 * D:3 * D], start=True, stop=True)
                        last = nc.tensor.matmul(gate(i, 3 * D, 4 * D), xt[:, col], w_hh[:, 2 * D:3 * D], start=True, stop=True)
                    last.then_inc(gates_ready, 1)
                pe.wait_ge(summed, z.NB)

            @block.vector
            def _(dve):
                v = nc.vector
                v.memset(xt[D:D + 1, :], 1.0).then_inc(ones_set, 1)
                v.memset(agg[D:D + 1, :], 1.0).then_inc(ones_set, 1)

                def tiles_of(x, tiles):
                    return x[:, 6, :] if tiles.start else x[:, 0:6, :].rearrange("p (a b) n -> p a b n", b=2)
                with dve.Fori(0, z.NB) as b:
                    dve.drain()
                    dve.wait_ge(rz_ready, b * 2 + 2)
                    for src, tiles in pairs(3 * D, 4 * D):
                        v.tensor_tensor(tiles_of(nn, tiles), src, tiles_of(rz[:, :, 0:D], tiles), ALU.mult)
                    dve.drain()
                    for (src, tiles), inc in zip(pairs(2 * D, 3 * D), (0, 1)):
                        last = v.tensor_tensor(tiles_of(nn, tiles), src, tiles_of(nn, tiles), ALU.add)
                    dve.drain().then_inc(n_ready, 1)
                    dve.wait_ge(n_done, b + 1)
                    v.tensor_tensor(y[:, :, :], block_of(k, b), nn[:, :, :], ALU.subtract)
                    dve.drain()
                    v.tensor_tensor(y[:, :, :], y[:, :, :], rz[:, :, D:2 * D], ALU.mult)
                    dve.drain()
                    v.tensor_tensor(y[:, :, :], y[:, :, :], nn[:, :, :], ALU.add)
                    dve.drain()
                    v.tensor_tensor(y[:, :, :], y[:, :, :], block_of(k, b), ALU.add)
                    norm_vector(nc, dve, k, y, s, b, eps_in, eps_out, done)


def build(nc, n, e, a, out):
    z = sizes(n, e)
    with ExitStack() as ctx:
        sb, ps, sem = make(nc, ctx)
        k = Names()
        k.x = sb("x_nodes", [P, z.NT * D])
        k.sq = sb("squares", [P, TB, D])
        k.acc0 = sb("acc0", [P, z.NC])
        k.ones = sb("ones", [P, P])
        k.ident = sb("ident", [P, P])
        k.before = sb("before", [P, P])
        k.after = sb("after", [P, P])
        k.pick = sb("pick", [2, 2, P], bf16)
        k.iota = sb("iota", [P, P])
        k.iota_p = sb("iota_p", [P, 1])
        k.src, k.dst, k.rel, k.src_hi, k.src_lo, k.dst_hi, k.dst_lo = (
            sb(m, [P, z.G * CH]) for m in ("src_pc", "dst_pc", "rel_pc", "src_hi", "src_lo", "dst_hi", "dst_lo"))
        k.table = sb("table", [1, z.G, 4], i32)
        k.table_limits = (z.n, -(-(z.n + 1) // W), z.G * (z.NT + 1))
        k.cnt_src = sb("cnt_src", [P, z.NT])
        k.cnt_dst = sb("cnt_dst", [P, z.NT])
        k.sync_groups = sem("sync_groups")
        k.pool_groups = sem("pool_groups")
        a["span_d"] = nc.dram_tensor("span_d", (z.G, 2), fp32).ap()
        a["hilo_d"] = nc.dram_tensor("hilo_d", (2, z.EP), bf16).ap()
        a["from_src_d"] = nc.dram_tensor("from_src_d", (z.NP, D), fp32).ap()
        a["from_dst_d"] = nc.dram_tensor("from_dst_d", (z.NC, 3 * D), bf16).ap()
        a["deg_d"] = nc.dram_tensor("deg_d", (z.NP,), fp32).ap()
        a["gains_d"] = nc.dram_tensor("gains_d", (z.NP, 4 * D), fp32).ap()
        a["sorted_d"] = nc.dram_tensor("sorted_d", (z.EP, RW), fp32).ap()
        a["scan_d"] = nc.dram_tensor("scan_d", (z.EP, 2 * F), fp32).ap()
        setup(nc, z, k, a)
        layer0_edges(nc, z, k, a)
        layer0_nodes(nc, z, k, a)
        layer1(nc, z, k, a)
        layer2(nc, z, k, a)
        layer3(nc, z, k, a)
        write_out(nc, z, k, out)


_TRANSPOSED = ('L3_gnn_W1', 'L3_gnn_W2', 'L3_gnn_w_ih', 'L3_gnn_w_hh')
_DATA = ['x', 'src', 'dst', 'edge_attr_32', 'edge_weight', 'edge_weight_n2']


def kernel(**inputs):
    import numpy as np
    import concourse.bacc as bacc
    from concourse import mybir as mb
    from concourse.bass_utils import run_bass_kernel_spmd as run

    n, e = inputs['x'].shape[0], inputs['src'].shape[0]
    z = sizes(n, e)

    def rows(array, count, fill):
        array = np.ascontiguousarray(array)
        padded = np.full((count,) + array.shape[1:], fill, array.dtype)
        padded[:array.shape[0]] = array
        return padded

    given = {
        'x': rows(inputs['x'], z.NP, 0),
        'src': rows(inputs['src'], z.EP, n),
        'dst': rows(inputs['dst'], z.EP, n),
        'w_low': rows(inputs['edge_weight'], z.EP, 0),
        'w_high': rows(inputs['edge_weight_n2'], z.EP, 0),
        'ea': rows(inputs['edge_attr_32'], z.EP, 0),
    }
    given['xT'] = np.ascontiguousarray(given['x'].T)
    given['eaT'] = np.ascontiguousarray(given['ea'].reshape(z.G, P, CH, F).transpose(0, 3, 2, 1).reshape(z.G, F, GE))
    for name in inputs:
        if name not in _DATA:
            w = np.ascontiguousarray(inputs[name])
            given[name] = np.ascontiguousarray(w.T) if name in _TRANSPOSED else w

    nc = bacc.Bacc("TRN2", target_bir_lowering=False, num_devices=1)
    arrays, a = {}, {}
    for name, array in given.items():
        arrays[f"in_{name}"] = array
        a[name] = nc.dram_tensor(f"in_{name}", array.shape, mb.dt.from_np(array.dtype), kind="ExternalInput").ap()
    out = nc.dram_tensor("out_x", (n, D), mb.dt.float32, kind="ExternalOutput").ap()
    build(nc, n, e, a, out)
    r = run(nc, [arrays], core_ids=[0])
    return r.results[0]["out_x"]
```
